# Optimizing a Trainium2 kernel written in Bass

```python
import numpy as np
import jax
import jax.numpy as jnp

def _softmax(x, axis=-1):
    return jax.nn.softmax(x, axis=axis)

def _gelu(x):
    return jax.nn.gelu(x, approximate=True)

def _silu(x):
    return jax.nn.silu(x)

def _sigmoid(x):
    return jax.nn.sigmoid(x)

def _layernorm(x, axis=-1, eps=1e-05):
    m = jnp.mean(x, axis=axis, keepdims=True)
    v = jnp.var(x, axis=axis, keepdims=True)
    return (x - m) / jnp.sqrt(v + eps)

def _scatter_add(tgt, idx, src, axis=0):
    return tgt.at[idx].add(src)

def _segment_sum(src, seg, n):
    return jax.ops.segment_sum(src, seg, n)
kernel_name = 'mk_gnn_resnorm_d1_gnn_r8_9c3e14'

def setup_inputs(seed: int=0):
    np.random.seed(seed)
    _w = jnp.asarray

    def _rec_inputs():
        import jax
        import jax.numpy as jnp
        _gk = jax.random.key(seed)
        x = -0.0008691 + 1 * jax.random.normal(jax.random.fold_in(_gk, 1), (6250, 128), jnp.float32)
        _s = jax.random.randint(jax.random.fold_in(_gk, 2), (100000,), 0, 6250, jnp.int32)
        _d = jax.random.randint(jax.random.fold_in(_gk, 3), (100000,), 0, 6250, jnp.int32)
        _loop = jnp.arange(6250, dtype=jnp.int32)
        src = jnp.concatenate([_s, _d, _loop])
        dst = jnp.concatenate([_d, _s, _loop])
        _o = jnp.argsort(dst, stable=True)
        src = src[_o]
        dst = dst[_o]
        edge_attr_128 = -8.513e-05 + 0.999844 * jax.random.normal(jax.random.fold_in(_gk, 12), (206250, 128), jnp.float32)
        return (x, src, dst, edge_attr_128)
    x, src, dst, edge_attr_128 = _rec_inputs()

    def _L0_gnn_setup():
        import jax, jax.numpy as jnp
        import numpy as np
        N_NODES = 1250
        N_EDGES = 80000
        D = 128
        key = jax.random.key(seed)
        ks = jax.random.split(key, 10)
        sc = 1.0 / np.sqrt(D)
        return {'node_features': jax.random.normal(ks[0], (N_NODES, D), jnp.float32), 'edge_features': jax.random.normal(ks[1], (N_EDGES, D), jnp.float32), 'src': jax.random.randint(ks[2], (N_EDGES,), 0, N_NODES), 'dst': jax.random.randint(ks[3], (N_EDGES,), 0, N_NODES), 'W_node': jax.random.normal(ks[4], (D, D), jnp.float32) * sc, 'b_node': jnp.zeros((D,), jnp.float32), 'W_edge': jax.random.normal(ks[5], (D, D), jnp.float32) * sc, 'b_edge': jnp.zeros((D,), jnp.float32), 'W_msg': jax.random.normal(ks[6], (D, D), jnp.float32) * sc, 'b_msg': jnp.zeros((D,), jnp.float32)}
    _L0_gnn_all = _L0_gnn_setup()
    _L0_gnn_in = {k: v for k, v in _L0_gnn_all.items() if k in ('W_node', 'b_node', 'W_edge', 'b_edge', 'W_msg', 'b_msg')}
    del _L0_gnn_all
    return {'x': x, 'src': src, 'dst': dst, 'edge_attr_128': edge_attr_128, 'L0_gnn_W_node': _L0_gnn_in['W_node'], 'L0_gnn_b_node': _L0_gnn_in['b_node'], 'L0_gnn_W_edge': _L0_gnn_in['W_edge'], 'L0_gnn_b_edge': _L0_gnn_in['b_edge'], 'L0_gnn_W_msg': _L0_gnn_in['W_msg'], 'L0_gnn_b_msg': _L0_gnn_in['b_msg']}

def reference(x, src, dst, edge_attr_128, L0_gnn_W_node, L0_gnn_b_node, L0_gnn_W_edge, L0_gnn_b_edge, L0_gnn_W_msg, L0_gnn_b_msg):
    import jax
    import jax.numpy as jnp

    def _L0_gnn_ref(node_features, edge_features, src, dst, W_node, b_node, W_edge, b_edge, W_msg, b_msg):
        import jax, jax.numpy as jnp
        import numpy as np
        N_NODES = 1250
        N_EDGES = 80000
        D = 128
        h = node_features @ W_node.T + b_node
        e = edge_features @ W_edge.T + b_edge
        msg = h[src] + e
        msg = msg @ W_msg.T + b_msg
        n = node_features.shape[0]
        s = jax.ops.segment_sum(msg, dst, num_segments=n)
        deg = jax.ops.segment_sum(jnp.ones(dst.shape, msg.dtype), dst, num_segments=n)
        return s / jnp.maximum(deg, 1.0)[:, None]
    x = _layernorm(x + _L0_gnn_ref(x, edge_attr_128, src, dst, L0_gnn_W_node, L0_gnn_b_node, L0_gnn_W_edge, L0_gnn_b_edge, L0_gnn_W_msg, L0_gnn_b_msg), axis=-1)
    return x

_drawn_inputs = setup_inputs


def setup_inputs(seed=0):
    import zlib

    import numpy as np

    out = dict(_drawn_inputs(seed))
    spreads = {'L0_gnn_b_node': (0.0, 0.1), 'L0_gnn_b_edge': (0.0, 0.1), 'L0_gnn_b_msg': (0.0, 0.1)}
    factors = {}
    for name, (base, spread) in spreads.items():
        noise = np.random.default_rng([zlib.crc32(name.encode()), seed]).standard_normal(out[name].shape)
        drawn = base * np.exp(spread * noise) if base else spread * noise
        out[name] = jnp.asarray(drawn.astype(out[name].dtype))
    for name, factor in factors.items():
        out[name] = (out[name] * factor).astype(out[name].dtype)
    return out
```

```python
from contextlib import ExitStack

import concourse.bass as bass
from concourse import mybir

ALU = mybir.AluOpType
ACT = mybir.ActivationFunctionType
AX = mybir.AxisListType
F32 = mybir.dt.float32
I32 = mybir.dt.int32

P = 128
D = 128
CH = 1024
J = CH // P
W = 64
SLOTS = 3
NB = 250
PB = NB // 2
EPS = 1e-5
FAR = -1.0e6


def gnn_layer(nc, x, src, dst, edge_attr, w_node, b_node, w_edge, b_edge, w_msg, b_msg, out):
    N = x.shape[0]
    E = edge_attr.shape[0]
    NFULL = E // CH
    REPEATED = CH - (E - NFULL * CH)
    ROUNDS = NFULL // SLOTS
    NCH = NFULL + 1
    NCOL = (ROUNDS + 1) * SLOTS
    WINDOWS = -(-N // W)
    NP = WINDOWS * W
    BLOCKS = N // NB
    assert NFULL % SLOTS == 0 and N % NB == 0 and E > CH

    with ExitStack() as ctx:
        def sb(name, shape, dt=F32):
            return ctx.enter_context(nc.sbuf_tensor(name, shape, dt))

        def sem(name):
            return ctx.enter_context(nc.semaphore(name))

        sums = sb("sums", [P, 3, NP])
        edges = sb("edges", [P, SLOTS, J, D])
        gathered = sb("gathered", [P, SLOTS, J, D])
        onehot = sb("onehot", [P, SLOTS, J, W])
        onehot_sum = sb("onehot_sum", [P, SLOTS, W])
        dst_int = sb("dst_int", [P, NCH, J], I32)
        src_int = sb("src_int", [P, NCH, J], I32)
        dst_col = sb("dst_col", [P, NCOL, J])
        rel_col = sb("rel_col", [P, NCOL, J])
        inside = sb("inside", [P, NCOL, J])
        first_row = sb("first_row", [1, NCH])
        last_int = sb("last_int", [1, 1], I32)
        base_row = sb("base_row", [1, NCH])
        base_int = sb("base_int", [1, NCH], I32)
        src_idx = sb("src_idx", [P, SLOTS, J], I32)
        iota_w = sb("iota_w", [P, W])
        iota_f = sb("iota_f", [P, P])
        iota_p = sb("iota_p", [P, 1])
        position = sb("position", [P, J])
        keep = sb("keep", [P, J])
        shifted = sb("shifted", [P, J])
        ident = sb("ident", [P, P])
        ones = sb("ones", [P, P])
        captured = sb("captured", [P, 1])
        flag_int = sb("flag_int", [1, 1], I32)
        weights = sb("weights", [P, 3, D])
        weights_t = sb("weights_t", [P, 3, D])
        bias_col = sb("bias_col", [P, 2])
        bias_ne = sb("bias_ne", [P, 1])
        bias_m = sb("bias_m", [1, D])
        fb_rel = sb("fb_rel", [P, J])
        recip = sb("recip", [P, NB])
        has_edge = sb("has_edge", [P, NB])
        scaled = sb("scaled", [P, NB])
        mean_in = sb("mean_in", [P, NB])
        resid = sb("resid", [PB, 2 * BLOCKS, D])
        stats = sb("stats", [PB, 2 * BLOCKS, 6])
        mean = sb("mean", [PB, 2 * BLOCKS])
        half_gap = sb("half_gap", [PB, 2 * BLOCKS])
        var_eps = sb("var_eps", [PB, 2 * BLOCKS])
        stddev = sb("stddev", [PB, 2 * BLOCKS])
        rstd = sb("rstd", [PB, 2 * BLOCKS])

        ps = [ctx.enter_context(nc.psum_tensor(f"ps{s}", [P, 512], F32)) for s in range(SLOTS)]
        ps_a = ctx.enter_context(nc.psum_tensor("ps_a", [P, 512], F32))
        ps_b = ctx.enter_context(nc.psum_tensor("ps_b", [P, 512], F32))

        dst_in = sem("dst_in")
        src_in = sem("src_in")
        first_in = sem("first_in")
        small_in = sem("small_in")
        consts = sem("consts")
        prep = sem("prep")
        dve_chain = sem("dve_chain")
        base_ready = sem("base_ready")
        base_bcast = sem("base_bcast")
        edge_in = [sem(f"edge_in{s}") for s in range(SLOTS)]
        idx_copied = [sem(f"idx_copied{s}") for s in range(SLOTS)]
        x_in = [sem(f"x_in{s}") for s in range(SLOTS)]
        onehot_ready = [sem(f"onehot_ready{s}") for s in range(SLOTS)]
        onehot_made = [sem(f"onehot_made{s}") for s in range(SLOTS)]
        fb_chain = sem("fb_chain")
        fb_moved = sem("fb_moved")
        fb_made = sem("fb_made")
        blk_step = sem("blk_step")
        chunk_mm = [sem(f"chunk_mm{s}") for s in range(SLOTS)]
        ps_free = [sem(f"ps_free{s}") for s in range(SLOTS)]
        cap_ready = sem("cap_ready")
        cap_sum = sem("cap_sum")
        flag_ready = sem("flag_ready")
        ident_ready = sem("ident_ready")
        wt_mm = sem("wt_mm")
        wt_ready = sem("wt_ready")
        fb_edge_in = sem("fb_edge_in")
        fb_idx = sem("fb_idx")
        fb_x_in = sem("fb_x_in")
        fb_onehot = sem("fb_onehot")
        fb_mm = sem("fb_mm")
        fb_added = sem("fb_added")
        fb_chunk_done = sem("fb_chunk_done")
        sums_ready = sem("sums_ready")
        blk_mean = sem("blk_mean")
        blk_mm1 = sem("blk_mm1")
        blk_mm2 = sem("blk_mm2")
        blk_resid = sem("blk_resid")
        stats_done = sem("stats_done")
        var_ready = sem("var_ready")
        std_ready = sem("std_ready")
        y_ready = sem("y_ready")
        out_done = sem("out_done")
        x_rows_in = sem("x_rows_in")

        full_edges = NFULL * CH
        edge_rows = edge_attr[0:full_edges, :].rearrange("(c p j) d -> c p j d", p=P, j=J)
        edge_last = edge_attr[E - CH:E, :].rearrange("(p j) d -> p j d", j=J)
        x_rows = x.rearrange("(g p h) d -> g p h d", p=PB, h=2)
        out_rows = out.rearrange("(g p h) d -> g p h d", p=PB, h=2)

        def load_index(eng, to, array, signal):
            eng.dma_start(to[:, 0:NFULL, :], array[0:full_edges].rearrange("(c p j) -> p c j", p=P, j=J)).then_inc(signal, 16)
            eng.dma_start(to[:, NFULL, :], array[E - CH:E].rearrange("(p j) -> p j", j=J)).then_inc(signal, 16)

        block = ctx.enter_context(nc.Block())

        @block.sync
        def _(sp):
            load_index(sp, dst_int, dst, dst_in)
            sp.dma_start(last_int[:, :], dst[full_edges:full_edges + 1].rearrange("(a b) -> a b", a=1)).then_inc(first_in, 16)
            load_index(sp, src_int, src, src_in)
            for n, w in enumerate((w_node, w_edge, w_msg)):
                sp.dma_start(weights[:, n, :], w).then_inc(small_in, 16)
            for n, b in enumerate((b_node, b_edge)):
                sp.dma_start(bias_col[:, n:n + 1], b.rearrange("(d a) -> d a", a=1)).then_inc(small_in, 16)
            sp.dma_start(resid[:, :, :].rearrange("p (g h) d -> p g h d", h=2), x_rows.rearrange("g p h d -> p g h d")).then_inc(x_rows_in, 16)
            sp.dma_start(bias_m[:, :], b_msg.rearrange("(a d) -> a d", a=1)).then_inc(small_in, 16)

            def load_chunk(s, n, rows):
                sp.wait_ge(chunk_mm[s], n + 1)
                sp.dma_start(edges[:, s, :, :], rows).then_inc(edge_in[s], 16)

            with sp.Fori(0, ROUNDS) as i:
                for s in range(SLOTS):
                    load_chunk(s, i, edge_rows[i * SLOTS + s])
            load_chunk(0, ROUNDS, edge_last)

            sp.wait_ge(flag_ready, 1)
            flag = sp.value_load(flag_int[0:1, 0:1], min_val=0, max_val=1)
            with sp.If(flag > 0):
                def fb_load(c, rows):
                    sp.wait_ge(fb_chunk_done, c + 1)
                    sp.dma_start(edges[:, 0, :, :], rows).then_inc(fb_edge_in, 16)
                with sp.Fori(0, NFULL) as c:
                    fb_load(c, edge_rows[c])
                fb_load(NFULL, edge_last)

        @block.gpsimd
        def _(pool):
            pool.iota(iota_w[:, :], pattern=[[1, W]], base=0, channel_multiplier=0,
                      allow_small_or_imprecise_dtypes=True).then_inc(consts, 1)
            pool.iota(iota_f[:, :], pattern=[[1, P]], base=0, channel_multiplier=0,
                      allow_small_or_imprecise_dtypes=True).then_inc(consts, 1)
            pool.iota(iota_p[:, :], pattern=[[0, 1]], base=0, channel_multiplier=1,
                      allow_small_or_imprecise_dtypes=True).then_inc(consts, 1)
            pool.iota(position[:, :], pattern=[[1, J]], base=0, channel_multiplier=J,
                      allow_small_or_imprecise_dtypes=True).then_inc(consts, 1)
            pool.wait_ge(src_in, 32)

            def gather(s, c, idx_done, idx_value, done):
                pool.tensor_copy(src_idx[:, s, :], src_int[:, bass.ds(c, 1), :].rearrange("p a j -> p (a j)")).then_inc(idx_done, 1)
                pool.wait_ge(src_in, 32)
                pool.wait_ge(idx_done, idx_value)
                for j in range(J):
                    pool.indirect_dma_start(
                        out=gathered[:, s, j, :], out_offset=None, in_=x[:, :],
                        in_offset=bass.IndirectOffsetOnAxis(ap=src_idx[:, s, j:j + 1], axis=0)).then_inc(done, 16)

            def gather_chunk(s, n, c):
                pool.wait_ge(chunk_mm[s], n + 1)
                gather(s, c, idx_copied[s], n + 1, x_in[s])

            with pool.Fori(0, ROUNDS) as i:
                for s in range(SLOTS):
                    gather_chunk(s, i, i * SLOTS + s)
            gather_chunk(0, ROUNDS, NFULL)

            pool.wait_ge(flag_ready, 1)
            flag = pool.value_load(flag_int[0:1, 0:1], min_val=0, max_val=1)
            with pool.If(flag > 0):
                with pool.Fori(0, NCH) as c:
                    pool.wait_ge(fb_chunk_done, c + 1)
                    gather(0, c, fb_idx, c + 1, fb_x_in)

        @block.tensor
        def _(pe):
            for s in range(SLOTS):
                pe.sem_inc(chunk_mm[s], 1)
            pe.wait_ge(small_in, 96)
            pe.wait_ge(ident_ready, 1)
            for n in range(3):
                mm = pe.transpose(ps_a[:, n * D:(n + 1) * D], weights[:, n, :], ident[:, :])
            mm.then_inc(wt_mm, 1)
            pe.wait_ge(base_ready, 1)
            pe.matmul(ps_b[:, 0:NCH], ones[0:1, :], base_row[:, :], start=True, stop=True).then_inc(base_bcast, 1)

            def chunk(s):
                for kind, rows in ((0, gathered), (1, edges)):
                    for j in range(J):
                        pe.matmul(ps[s][:, kind * W:(kind + 1) * W], rows[:, s, j, :], onehot[:, s, j, :],
                                  start=(j == 0), stop=(j == J - 1))
                return pe.matmul(ps[s][:, 2 * W:3 * W], ones[:, :], onehot_sum[:, s, :], start=True, stop=True)

            def main_chunk(s, n):
                pe.wait_ge(onehot_ready[s], n + 1)
                pe.wait_ge(ps_free[s], n + 1)
                pe.wait_ge(edge_in[s], (n + 1) * 16)
                pe.wait_ge(x_in[s], (n + 1) * (16 * J))
                chunk(s).then_inc(chunk_mm[s], 1)

            with pe.Fori(0, ROUNDS) as i:
                for s in range(SLOTS):
                    main_chunk(s, i)
            main_chunk(0, ROUNDS)

            pe.wait_ge(cap_ready, 1)
            pe.matmul(ps_b[:, 0:1], ones[:, :], captured[:, :], start=True, stop=True).then_inc(cap_sum, 1)

            pe.wait_ge(flag_ready, 1)
            flag = pe.value_load(flag_int[0:1, 0:1], min_val=0, max_val=1)
            with pe.If(flag > 0):
                with pe.Fori(0, NCH) as c:
                    with pe.Fori(0, WINDOWS) as w:
                        pe.wait_ge(fb_edge_in, (c + 1) * 16)
                        pe.wait_ge(fb_x_in, (c + 1) * (16 * J))
                        pe.wait_ge(fb_onehot, c * WINDOWS + w + 1)
                        chunk(0).then_inc(fb_mm, 1)

            pe.wait_ge(sums_ready, 1)
            with pe.Fori(0, BLOCKS) as g:
                pe.wait_ge(blk_mean, g + 1)
                pe.matmul(ps_a[:, 0:NB], weights_t[:, 0, :], sums[:, 0, bass.ds(g * NB, NB)], start=True, stop=False)
                pe.matmul(ps_a[:, 0:NB], weights_t[:, 1, :], sums[:, 1, bass.ds(g * NB, NB)],
                          start=False, stop=True).then_inc(blk_mm1, 1)
                pe.wait_ge(blk_mean, g + 2)
                pe.wait_ge(blk_resid, g + 1)
                for h in range(2):
                    pe.matmul(ps_b[0:PB, h * D:(h + 1) * D], mean_in[:, h:NB:2], weights_t[:, 2, :], start=True, stop=False)
                    mm = pe.matmul(ps_b[0:PB, h * D:(h + 1) * D], has_edge[0:1, h:NB:2], bias_m[:, :], start=False, stop=True)
                mm.then_inc(blk_mm2, 1)

        @block.vector
        def _(dve):
            steps = [0]

            def link(ins):
                steps[0] += 1
                ins.then_inc(dve_chain, 1)
                dve.wait_ge(dve_chain, steps[0])

            for s in range(SLOTS):
                dve.sem_inc(ps_free[s], 1)
            dve.memset(ones[:, :], 1.0)
            dve.memset(rel_col[:, :, :], FAR)
            link(dve.memset(sums[:, :, :], 0.0))
            dve.wait_ge(consts, 4)
            dve.tensor_scalar(ident[:, :], iota_f[:, :], iota_p[:, 0:1], None, ALU.is_equal).then_inc(ident_ready, 1)
            dve.wait_ge(dst_in, 32)
            dve.wait_ge(first_in, 16)
            link(dve.tensor_copy(dst_col[:, 0:NCH, :], dst_int[:, :, :]))
            link(dve.tensor_scalar(keep[:, :], position[:, :], float(REPEATED), None, ALU.is_ge))
            link(dve.tensor_scalar(shifted[:, :], dst_col[:, NFULL, :], -FAR, None, ALU.add))
            link(dve.tensor_tensor(shifted[:, :], shifted[:, :], keep[:, :], ALU.mult))
            link(dve.tensor_scalar(dst_col[:, NFULL, :], shifted[:, :], FAR, None, ALU.add))
            dve.tensor_copy(first_row[:, 0:NFULL], dst_col[0:1, 0:NFULL, 0])
            link(dve.tensor_copy(first_row[:, NFULL:NCH], last_int[:, :]))
            link(dve.tensor_scalar(base_row[:, :], first_row[:, :], float(NP - W), 0.0, ALU.min, ALU.max))
            link(dve.tensor_copy(base_int[:, :], base_row[:, :]))
            dve.sem_inc(base_ready, 1)
            dve.wait_ge(base_bcast, 1)
            link(dve.tensor_tensor(rel_col[:, 0:NCH, :], dst_col[:, 0:NCH, :],
                                   ps_b[:, 0:NCH].rearrange("p (c a) -> p c a", a=1).to_broadcast([P, NCH, J]), ALU.subtract))
            dve.wait_ge(wt_mm, 1)
            dve.tensor_copy(weights_t[:, :, :], ps_a[:, 0:3 * D].rearrange("p (n d) -> p n d", n=3))
            dve.tensor_tensor(bias_ne[:, :], bias_col[:, 0:1], bias_col[:, 1:2], ALU.add)
            link(dve.tensor_scalar(inside[:, :, :], rel_col[:, :, :], 0.0, None, ALU.is_ge))
            dve.scalar_tensor_tensor(inside[:, :, :], rel_col[:, :, :], float(W), inside[:, :, :], ALU.is_lt, ALU.mult,
                                     accum_out=captured[:, :]).then_inc(cap_ready, 1)

            def main_onehot(s, n, c):
                dve.tensor_tensor(onehot[:, s, :, :], iota_w[:, :].rearrange("p (a w) -> p a w", a=1).to_broadcast([P, J, W]),
                                  rel_col[:, bass.ds(c, 1), :].rearrange("p a j -> p j a").to_broadcast([P, J, W]),
                                  ALU.is_equal).then_inc(onehot_made[s], 1)
                dve.wait_ge(onehot_made[s], n + 1)
                dve.tensor_reduce(onehot_sum[:, s, :], onehot[:, s, :, :].rearrange("p j w -> p w j"), AX.X,
                                  ALU.add).then_inc(onehot_ready[s], 1)

            def add_sums(s, at):
                return dve.tensor_tensor(sums[:, :, bass.ds(at, W)], sums[:, :, bass.ds(at, W)],
                                         ps[s][:, 0:3 * W].rearrange("p (k w) -> p k w", k=3), ALU.add)

            def main_add(s, n, c):
                at = dve.value_load(base_int[0:1, bass.ds(c, 1)], min_val=0, max_val=NP - W)
                dve.wait_ge(chunk_mm[s], n + 2)
                before = (s - 1) % SLOTS
                dve.wait_ge(ps_free[before], n + (2 if s else 1))
                add_sums(s, at).then_inc(ps_free[s], 1)

            for s in range(SLOTS):
                main_onehot(s, 0, s)
            with dve.Fori(0, ROUNDS) as i:
                for s in range(SLOTS):
                    main_add(s, i, i * SLOTS + s)
                    main_onehot(s, i + 1, i * SLOTS + s + SLOTS)
            main_add(0, ROUNDS, NFULL)

            dve.wait_ge(cap_sum, 1)
            dve.tensor_scalar(flag_int[:, :], ps_b[0:1, 0:1], float(E), None, ALU.not_equal).then_inc(flag_ready, 1)
            dve.wait_ge(flag_ready, 1)
            dve.wait_ge(ps_free[0], ROUNDS + 2)
            flag = dve.value_load(flag_int[0:1, 0:1], min_val=0, max_val=1)
            with dve.If(flag > 0):
                dve.memset(sums[:, :, :], 0.0).then_inc(fb_chain, 1)
                dve.wait_ge(fb_chain, 1)
                dve.sem_inc(fb_chunk_done, 1)
                with dve.Fori(0, NCH) as c:
                    dve.tensor_copy(fb_rel[:, :], dst_col[:, bass.ds(c, 1), :].rearrange("p a j -> p (a j)")).then_inc(fb_moved, 1)
                    with dve.Fori(0, WINDOWS) as w:
                        n = c * WINDOWS + w
                        dve.wait_ge(fb_moved, n + c + 1)
                        dve.tensor_tensor(onehot[:, 0, :, :], iota_w[:, :].rearrange("p (a w) -> p a w", a=1).to_broadcast([P, J, W]),
                                          fb_rel[:, :].rearrange("p (j a) -> p j a", a=1).to_broadcast([P, J, W]),
                                          ALU.is_equal).then_inc(fb_made, 1)
                        dve.wait_ge(fb_made, n + 1)
                        dve.tensor_reduce(onehot_sum[:, 0, :], onehot[:, 0, :, :].rearrange("p j w -> p w j"), AX.X,
                                          ALU.add).then_inc(fb_onehot, 1)
                        dve.tensor_scalar(fb_rel[:, :], fb_rel[:, :], -float(W), None, ALU.add).then_inc(fb_moved, 1)
                        dve.wait_ge(fb_mm, n + 1)
                        add_sums(0, w * W).then_inc(fb_added, 1)
                        dve.wait_ge(fb_added, n + 1)
                    dve.sem_inc(fb_chunk_done, 1)

            dve.sem_inc(sums_ready, 1)
            dve.sem_inc(blk_mean, 1)
            dve.sem_inc(blk_resid, 1)
            dve.wait_ge(x_rows_in, 16)
            with dve.Fori(0, BLOCKS) as g:
                deg = sums[:, 2, bass.ds(g * NB, NB)]
                dve.tensor_scalar(recip[:, :], deg, 1.0, None, ALU.max).then_inc(blk_step, 1)
                dve.wait_ge(blk_step, g * 4 + 1)
                dve.reciprocal(recip[:, :], recip[:, :]).then_inc(blk_step, 1)
                dve.wait_ge(blk_resid, g + 1)
                dve.tensor_scalar(has_edge[:, :], deg, 1.0, None, ALU.min).then_inc(blk_step, 1)
                dve.wait_ge(blk_step, g * 4 + 3)
                dve.wait_ge(blk_mm1, g + 1)
                dve.tensor_tensor(scaled[:, :], ps_a[:, 0:NB], recip[:, :], ALU.mult).then_inc(blk_step, 1)
                dve.wait_ge(blk_step, g * 4 + 4)
                dve.scalar_tensor_tensor(mean_in[:, :], has_edge[:, :], bias_ne[:, 0:1], scaled[:, :],
                                         ALU.mult, ALU.add).then_inc(blk_mean, 1)
                dve.wait_ge(blk_mm2, g + 1)
                dve.tensor_tensor(resid[:, bass.ds(g * 2, 2), :], resid[:, bass.ds(g * 2, 2), :],
                                  ps_b[0:PB, 0:2 * D].rearrange("p (h d) -> p h d", h=2), ALU.add).then_inc(blk_resid, 1)
                dve.wait_ge(blk_resid, g + 2)
                for h in range(2):
                    dve.bn_stats(stats[:, bass.ds(g * 2 + h, 1), :].rearrange("p a s -> p (a s)"),
                                 resid[:, bass.ds(g * 2 + h, 1), :].rearrange("p a d -> p (a d)")).then_inc(stats_done, 1)

            dve.wait_ge(stats_done, BLOCKS * 2)
            dve.tensor_tensor(mean[:, :], stats[:, :, 1], stats[:, :, 4], ALU.add)
            dve.tensor_tensor(half_gap[:, :], stats[:, :, 1], stats[:, :, 4], ALU.subtract)
            link(dve.tensor_tensor(var_eps[:, :], stats[:, :, 2], stats[:, :, 5], ALU.add))
            dve.tensor_scalar(mean[:, :], mean[:, :], 0.5, None, ALU.mult)
            dve.tensor_scalar(var_eps[:, :], var_eps[:, :], 1.0 / D, EPS, ALU.mult, ALU.add)
            link(dve.tensor_scalar(half_gap[:, :], half_gap[:, :], 0.5, None, ALU.mult))
            link(dve.tensor_tensor(half_gap[:, :], half_gap[:, :], half_gap[:, :], ALU.mult))
            dve.tensor_tensor(var_eps[:, :], var_eps[:, :], half_gap[:, :], ALU.add).then_inc(var_ready, 1)
            dve.wait_ge(std_ready, 1)
            link(dve.reciprocal(rstd[:, :], stddev[:, :]))
            with dve.Fori(0, BLOCKS) as g:
                for h in range(2):
                    at = g * 2 + h
                    row = resid[:, bass.ds(at, 1), :].rearrange("p a d -> p (a d)")
                    dve.tensor_scalar(row, row, mean[:, bass.ds(at, 1)], rstd[:, bass.ds(at, 1)],
                                      ALU.subtract, ALU.mult).then_inc(y_ready, 1)

        @block.scalar
        def _(act):
            act.wait_ge(var_ready, 1)
            act.activation(stddev[:, :], var_eps[:, :], ACT.Sqrt).then_inc(std_ready, 1)
            with act.Fori(0, BLOCKS) as g:
                act.wait_ge(y_ready, (g + 1) * 2)
                act.dma_start(out_rows[g], resid[:, bass.ds(g * 2, 2), :]).then_inc(out_done, 16)
            act.wait_ge(out_done, BLOCKS * 16)


_INS = ["x", "src", "dst", "edge_attr_128", "L0_gnn_W_node", "L0_gnn_b_node", "L0_gnn_W_edge", "L0_gnn_b_edge",
        "L0_gnn_W_msg", "L0_gnn_b_msg"]


def kernel(**inputs):
    import numpy as _np
    import concourse.bacc as _bacc
    from concourse import mybir as _mybir
    from concourse.bass_utils import run_bass_kernel_spmd as _run

    nc = _bacc.Bacc("TRN2", target_bir_lowering=False, num_devices=1)
    arrays, args = {}, []
    for name in _INS:
        a = _np.ascontiguousarray(inputs[name])
        arrays[f"in_{name}_dram"] = a
        args.append(nc.dram_tensor(f"in_{name}_dram", a.shape, _mybir.dt.from_np(a.dtype), kind="ExternalInput").ap())
    out = nc.dram_tensor("out_dram", inputs["x"].shape, _mybir.dt.float32, kind="ExternalOutput").ap()
    gnn_layer(nc, *args, out)
    r = _run(nc, [arrays], core_ids=[0])
    return r.results[0]["out_dram"]
```

```python
from contextlib import ExitStack

import concourse.bass as bass
from concourse import mybir

ALU = mybir.AluOpType
ACT = mybir.ActivationFunctionType
AX = mybir.AxisListType
F32 = mybir.dt.float32
BF16 = mybir.dt.bfloat16
I32 = mybir.dt.int32

P = 128
D = 128
EPS = 1e-5

CH = 1024
J = CH // P
W = 64

WN = 2
WE = 125
NB = 250
PB = NB // WN
BATCH = 25
SEGS = PB // BATCH
FILL = 5
FILLS = BATCH // FILL
ROW = 550

A_ROUND, B_ROUND = 4, 8
SEG_CHUNKS = [[("A", 0), ("B", 0), ("B", 1)], [("A", 1), ("B", 2), ("B", 3)], [("A", 2), ("B", 4), ("B", 5)],
              [("A", 3), ("B", 6)], [("B", 7)]]
PER_ROUND = A_ROUND + B_ROUND
EDGE_SLOTS = 3
ONEHOT_SLOTS = 3
GATHER_SLOTS = 2
CHUNK_BANKS = 2
M_BANKS = 4
SPLIT_BLOCKS = 7


def gnn_layer(nc, x, src, dst, edge_attr, w_node, b_node, w_edge, b_edge, w_msg, b_msg, out):
    N = x.shape[0]
    E = edge_attr.shape[0]
    NFULL = E // CH
    OWN = NFULL * CH
    REPEATED = CH - (E - OWN)
    NCH = NFULL + 1
    GROUPS = N // NB
    ROUNDS = (2 * GROUPS + 1) // 3
    G0 = GROUPS - ROUNDS
    CA = A_ROUND * ROUNDS
    LAST_B = NCH - CA - B_ROUND * (ROUNDS - 1)
    PAIRS = (ROUNDS - 3) // 2
    XB = -(-N // P)
    KEYS = WN * XB
    KPAD = -(-KEYS // 4) * 4
    WINDOWS = -(-N // W)
    NP = WINDOWS * W
    NROW = E // ROW
    T1 = NCH - P
    assert N % NB == 0 and NB % WN == 0 and FILL * KEYS <= 512
    assert 1 <= LAST_B <= B_ROUND and G0 == 1 + PAIRS, (ROUNDS, G0, LAST_B)
    assert CA <= P and CA * CH * N >= (G0 * NB + 50) * E
    assert E % ROW == 0 and E % WE == 0 and NROW <= 512 and WE <= P

    with ExitStack() as ctx:
        def sb(name, shape, dt=F32):
            return ctx.enter_context(nc.sbuf_tensor(name, shape, dt))

        def psum(name):
            return ctx.enter_context(nc.psum_tensor(name, [P, 512], F32))

        def sem(name):
            return ctx.enter_context(nc.semaphore(name))

        sums = sb("sums", [P, 2, NP])
        x_parts = sb("x_parts", [P, 3, XB, D], BF16)
        COUNTS = XB * NB
        region = sb("region", [P, COUNTS // 2 + max(COUNTS // 2, WN * GROUPS * D, XB * D)])
        degree = sb("degree", [PB, WN * GROUPS])
        captured = sb("captured", [P, 2 + ROUNDS])

        HALF = COUNTS // 2
        slot0, slot1 = region[:, 0:HALF], region[:, HALF:]
        counts = [region[:, k * HALF:(k + 1) * HALF].bitcast(BF16).rearrange("p (b n) -> p b n", b=XB) for k in range(2)]
        place = [0]

        def early(n, dt=F32):
            at = place[0]
            place[0] += n
            assert place[0] <= HALF
            return region[:, at:at + n].bitcast(dt) if dt != F32 else region[:, at:at + n]

        dst_nat = early(2 * CH, I32).rearrange("p (t e) -> p t e", t=2)
        rel_nat = early(CH, BF16).rearrange("p (t e) -> p t e", t=2)
        penalty = early(CH)
        firsts_int = early(NROW, I32)[0:1, :]
        chunk_firsts = early(NCH, I32)[0:1, :]
        weights = early(3 * D).rearrange("p (n d) -> p n d", n=3)
        wm_t = early(D)
        bias_rep = early(P)
        firsts = early(NROW)
        scratch = early(NROW)
        x_raw = slot1[:, 0:XB * D]
        resid = slot1[0:PB, 0:WN * GROUPS * D].rearrange("p (k d) -> p k d", d=D)

        edges = sb("edges", [P, EDGE_SLOTS, J, D])
        gathered = sb("gathered", [P, GATHER_SLOTS, J, D])
        onehot = sb("onehot", [P, ONEHOT_SLOTS, J, W])
        row_hot = sb("row_hot", [P, 2, BATCH, P], BF16)
        key_hot = sb("key_hot", [P, 2, BATCH, KPAD], BF16)
        row4 = sb("row4", [P, 2, PB, 4], BF16)
        key4 = sb("key4", [P, 2, PB, 4], BF16)
        rel_col = sb("rel_col", [P, NCH, J], BF16)
        src_col = sb("src_col", [P, CA, J], I32)
        src_idx = sb("src_idx", [P, GATHER_SLOTS, J], I32)
        base_int = sb("base_int", [1, NCH], I32)
        first_col_int = sb("first_col_int", [P, 2], I32)
        first_col = sb("first_col", [P, 2])
        is_last = sb("is_last", [P, 1])

        window_node = sb("window_node", [PB, GROUPS + 1])
        node_half = sb("node_half", [PB, GROUPS + 1])
        row_count = sb("row_count", [PB, GROUPS + 1])
        row_start = sb("row_start", [PB, GROUPS + 1])
        row_start_int = sb("row_start_int", [PB, GROUPS + 1], I32)
        row_middle = sb("row_middle", [PB, GROUPS + 1])
        row_idx = sb("row_idx", [PB, 1], I32)
        rows = sb("rows", [PB, ROW], I32)
        row_signs = sb("row_signs", [PB, ROW], BF16)
        sign_sum = sb("sign_sum", [PB, 1])
        start_tmp = sb("start_tmp", [PB, 1])
        start = [sb(f"start{k}", [PB, 1]) for k in range(2)]
        start_int = [sb(f"start_int{k}", [PB, 1], I32) for k in range(2)]
        win_dst = [sb(f"win_dst{k}", [PB, WE], I32) for k in range(2)]
        win_src = sb("win_src", [PB, WE], I32)
        src_block = sb("src_block", [PB, WE], I32)
        src_row = sb("src_row", [PB, WE], I32)
        rel_key = sb("rel_key", [PB, WE])
        early_edge = sb("early_edge", [PB, WE])
        key = sb("key", [PB, WE])
        key_bf = sb("key_bf", [PB, WE], BF16)
        row_bf = sb("row_bf", [PB, WE], BF16)
        held = sb("held", [PB, WN + 1, WE], BF16)

        iota_bf = sb("iota_bf", [P, P], BF16)
        iota_we = sb("iota_we", [P, P])
        iota_p = sb("iota_p", [P, 1])
        ident = sb("ident", [P, P])
        ident_bf = sb("ident_bf", [P, P], BF16)
        ones = sb("ones", [P, P])
        w_both = sb("w_both", [P, 2, D])
        bias_col = sb("bias_col", [P, 2])
        bias_m = sb("bias_m", [1, D])
        bias_row = sb("bias_row", [PB, D])
        totals = sb("totals", [1, 4])
        flag_int = sb("flag_int", [1, 1], I32)

        late_words = gathered[0:PB, 1, :, :].rearrange("p j d -> p (j d)")
        late_names = ("mean", "half_gap", "var_eps", "stddev", "rstd", "recip", "has_edge")
        mean, half_gap, var_eps, stddev, rstd, recip, has_edge = (
            late_words[:, k * WN * GROUPS:(k + 1) * WN * GROUPS] for k in range(len(late_names)))
        stats = late_words[:, len(late_names) * WN * GROUPS:(len(late_names) + 6) * WN * GROUPS].rearrange("p (k s) -> p k s", s=6)
        applied = [edges[:, k, :, :].rearrange("p j d -> p (j d)")[:, 0:NB] for k in range(2)]

        fb_row_int = edges[0:PB, 1, :, :].rearrange("p j d -> p (j d)").bitcast(I32)
        fb_row = edges[0:PB, 2, :, :].rearrange("p j d -> p (j d)")
        fb_equal = gathered[0:PB, 1, :, :].rearrange("p j d -> p (j d)")
        fb_dst_int = src_col[:, 0, :]
        fb_src_int = src_col[:, 1, :]
        fb_rel = sb("fb_rel", [P, J])[:, :]
        fb_pos = sb("fb_pos", [P, J])[:, :]
        fb_node = sb("fb_node", [PB, WN * GROUPS])[:, :]

        chunk_ps = [psum(f"chunk_ps{k}") for k in range(CHUNK_BANKS)]
        count_ps = [psum(f"count_ps{k}") for k in range(M_BANKS)]
        x_ps = psum("x_ps")
        turn_ps = psum("turn_ps")

        firsts_in = sem("firsts_in")
        dst_in = sem("dst_in")
        src_first_in = sem("src_first_in")
        src_in = sem("src_in")
        x_raw_in = sem("x_raw_in")
        small_in = sem("small_in")
        consts = sem("consts")
        ident_ready = sem("ident_ready")
        firsts_ready = sem("firsts_ready")
        firsts_spread = sem("firsts_spread")
        rel_nat_ready = sem("rel_nat_ready")
        rel_turned = sem("rel_turned")
        wm_turned = sem("wm_turned")
        wm_ready = sem("wm_ready")
        weights_mm = sem("weights_mm")
        prologue_done = sem("prologue_done")
        offsets_ready = sem("offsets_ready")
        x_zeroed = sem("x_zeroed")
        x_hi = sem("x_hi")
        x_rest = sem("x_rest")
        x_mid = sem("x_mid")
        x_lo = sem("x_lo")
        dve_chain = sem("dve_chain")

        edge_in = [sem(f"edge_in{k}") for k in range(EDGE_SLOTS)]
        idx_copied = sem("idx_copied")
        x_in = [sem(f"x_in{k}") for k in range(GATHER_SLOTS)]
        onehot_ready = sem("onehot_ready")
        chunk_done = sem("chunk_done")
        chunk_added = sem("chunk_added")

        row_idx_set = sem("row_idx_set")
        passed = sem("passed")
        row_in = sem("row_in")
        row_counted = sem("row_counted")
        start_step = sem("start_step")
        start_ready = [sem(f"start_ready{k}") for k in range(2)]
        win_in = [sem(f"win_in{k}") for k in range(2)]
        key_step = sem("key_step")
        keys_ready = sem("keys_ready")
        keys_used = sem("keys_used")
        degree_step = sem("degree_step")
        keys_turned = sem("keys_turned")
        keys_spread = sem("keys_spread")
        hots_ready = sem("hots_ready")
        bank_filled = sem("bank_filled")
        bank_moved = sem("bank_moved")
        x_mm = sem("x_mm")
        x_added = sem("x_added")

        caps_ready = sem("caps_ready")
        caps_summed = sem("caps_summed")
        flag_ready = sem("flag_ready")
        fb_edge_in = sem("fb_edge_in")
        fb_col_in = sem("fb_col_in")
        fb_row_in = sem("fb_row_in")
        fb_x_in = sem("fb_x_in")
        fb_chain = sem("fb_chain")
        fb_chain2 = sem("fb_chain2")
        tail_step = sem("tail_step")
        only_step = sem("only_step")
        fb_moved = sem("fb_moved")
        fb_onehot = sem("fb_onehot")
        fb_mm = sem("fb_mm")
        fb_added = sem("fb_added")
        fb_counted = sem("fb_counted")
        fb_chunk_done = sem("fb_chunk_done")
        resid_free = sem("resid_free")
        resid_in = sem("resid_in")
        resid_biased = sem("resid_biased")
        sums_ready = sem("sums_ready")
        applied_mm = sem("applied_mm")
        applied_moved = sem("applied_moved")
        applied_turned = sem("applied_turned")
        resid_ready = sem("resid_ready")
        stats_done = sem("stats_done")
        var_ready = sem("var_ready")
        std_ready = sem("std_ready")
        y_ready = sem("y_ready")
        out_done = sem("out_done")

        edge_rows = edge_attr[0:OWN, :].rearrange("(c p j) d -> c p j d", p=P, j=J)
        edge_last = edge_attr[E - CH:E, :].rearrange("(p j) d -> p j d", j=J)
        dst_chunks = dst[0:OWN].rearrange("(c e) -> c e", e=CH)
        src_chunks = src[0:OWN].rearrange("(c e) -> c e", e=CH)
        x_pairs = x.rearrange("(g p h) d -> p g h d", p=PB, h=WN)
        out_pairs = out.rearrange("(g p h) d -> g p h d", p=PB, h=WN)

        def at_least(eng, s, n):
            if not isinstance(n, int) or n > 0:
                eng.wait_ge(s, n)

        def in_turn(eng, count, step):
            step(0, 0, 0, False)
            step(1, 0, 1, False)
            with eng.Fori(0, (count - 3) // 2) as i:
                step(i * 2 + 2, i + 1, 0, False)
                step(i * 2 + 3, i + 1, 1, False)
            step(count - 1, (count - 1) // 2, 0, True)

        def chunks_of(last):
            segs, pos = [], 0
            for seg in SEG_CHUNKS:
                mine = []
                for kind, n in seg:
                    if kind == "A" or not last or n < LAST_B:
                        mine.append((kind, n, pos))
                        pos += 1
                segs.append(mine)
            return segs

        def chunk_id(m, kind, n):
            return m * A_ROUND + n if kind == "A" else m * B_ROUND + n + CA

        def after(m, last, pos, ahead):
            flat = [c for seg in chunks_of(last) for c in seg]
            if pos + ahead < len(flat):
                kind, n, _ = flat[pos + ahead]
                return m, kind, n
            if last:
                return None
            kind, n, _ = [c for seg in chunks_of(False) for c in seg][pos + ahead - len(flat)]
            return m + 1, kind, n

        A_POS = [pos for seg in chunks_of(False) for kind, n, pos in seg if kind == "A"]
        BLOCK_CUTS = [XB * s // SEGS for s in range(SEGS + 1)]

        def rows_before(half, odd):
            return half * 3 + (4 if odd else 2)

        block = ctx.enter_context(nc.Block())

        @block.sync
        def _(sp):
            sp.dma_start(src_col[:, 0:A_ROUND, :], src[0:A_ROUND * CH].rearrange("(c p j) -> p c j", p=P, j=J)).then_inc(src_first_in, 16)
            with nc.allow_non_contiguous_dma(reason="single destinations at a stride"):
                sp.dma_start(firsts_int.rearrange("a (r e) -> a r e", e=1), dst.rearrange("(a r e) -> a r e", a=1, e=ROW)[:, :, 0:1]).then_inc(firsts_in, 16)
                sp.dma_start(chunk_firsts[:, 0:NFULL].rearrange("a (r e) -> a r e", e=1), dst[0:OWN].rearrange("(a r e) -> a r e", a=1, e=CH)[:, :, 0:1]).then_inc(firsts_in, 16)
            sp.dma_start(chunk_firsts[:, NFULL:NCH], dst[OWN:OWN + 1].rearrange("(a b) -> a b", a=1)).then_inc(firsts_in, 16)
            sp.dma_start(dst_nat[:, 0, :], dst[0:P * CH].rearrange("(c e) -> c e", e=CH)).then_inc(dst_in, 16)
            sp.dma_start(dst_nat[0:T1 - 1, 1, :], dst[P * CH:OWN].rearrange("(c e) -> c e", e=CH)).then_inc(dst_in, 16)
            sp.dma_start(dst_nat[T1 - 1:T1, 1, :], dst[E - CH:E].rearrange("(c e) -> c e", e=CH)).then_inc(dst_in, 16)
            with nc.allow_non_contiguous_dma(reason="single destinations at a stride"):
                sp.dma_start(first_col_int[:, 0:1], dst[0:P * CH].rearrange("(c e) -> c e", e=CH)[:, 0:1]).then_inc(dst_in, 16)
            with nc.allow_non_contiguous_dma(reason="single destinations at a stride"):
                sp.dma_start(first_col_int[0:T1 - 1, 1:2], dst[P * CH:OWN].rearrange("(c e) -> c e", e=CH)[:, 0:1]).then_inc(dst_in, 16)
            sp.dma_start(first_col_int[T1 - 1:T1, 1:2], dst[OWN:OWN + 1].rearrange("(a b) -> a b", a=1)).then_inc(dst_in, 16)

            def load(m, half, odd, last):
                for seg in chunks_of(last):
                    for kind, n, pos in seg:
                        t = m * PER_ROUND + pos
                        k = pos % EDGE_SLOTS
                        at_least(sp, chunk_done, t - EDGE_SLOTS + 1)
                        final = last and kind == "B" and n == LAST_B - 1
                        sp.dma_start(edges[:, k, :, :], edge_last if final else edge_rows[chunk_id(m, kind, n)]).then_inc(edge_in[k], 16)
                        if isinstance(m, int) and m == 0 and pos == 1:
                            sp.dma_start(src_col[:, A_ROUND:CA, :], src[A_ROUND * CH:CA * CH].rearrange("(c p j) -> p c j", p=P, j=J)).then_inc(src_in, 16)
                            sp.wait_ge(x_zeroed, 1)
                            whole = N // P
                            sp.dma_start(x_raw[:, 0:whole * D].rearrange("p (b d) -> p b d", d=D), x[0:whole * P, :].rearrange("(b p) d -> p b d", p=P)).then_inc(x_raw_in, 16)
                            sp.dma_start(x_raw[0:N - whole * P, whole * D:XB * D], x[whole * P:N, :]).then_inc(x_raw_in, 16)
                            for w, a in enumerate((w_node, w_edge, w_msg)):
                                sp.dma_start(weights[:, w, :], a).then_inc(small_in, 16)
                            for w, a in enumerate((b_node, b_edge)):
                                sp.dma_start(bias_col[:, w:w + 1], a.rearrange("(d a) -> d a", a=1)).then_inc(small_in, 16)
                            sp.dma_start(bias_m[:, :], b_msg.rearrange("(a d) -> a d", a=1)).then_inc(small_in, 16)

            in_turn(sp, ROUNDS, load)
            sp.wait_ge(x_mm, ROUNDS - 1)
            sp.dma_start(resid.rearrange("p (g h) d -> p g h d", h=WN), x_pairs).then_inc(resid_in, 16)

            sp.wait_ge(flag_ready, 1)
            flag = sp.value_load(flag_int[0:1, 0:1], min_val=0, max_val=1)
            with sp.If(flag > 0):
                def fb_load(c, edge_part, dst_part, src_part):
                    sp.wait_ge(fb_chunk_done, c + 1)
                    sp.dma_start(edges[:, 0, :, :], edge_part).then_inc(fb_edge_in, 16)
                    sp.dma_start(fb_dst_int, dst_part.rearrange("a (p j) -> p (a j)", j=J)).then_inc(fb_col_in, 16)
                    sp.dma_start(fb_src_int, src_part.rearrange("a (p j) -> p (a j)", j=J)).then_inc(fb_col_in, 16)
                    sp.dma_start(fb_row_int, dst_part.to_broadcast([PB, CH])).then_inc(fb_row_in, 16)
                with sp.Fori(0, NFULL) as c:
                    fb_load(c, edge_rows[c], dst_chunks[bass.ds(c, 1), :], src_chunks[bass.ds(c, 1), :])
                fb_load(NFULL, edge_last, dst[E - CH:E].rearrange("(a e) -> a e", a=1), src[E - CH:E].rearrange("(a e) -> a e", a=1))

        @block.gpsimd
        def _(pool):
            pool.iota(iota_bf[:, :], pattern=[[1, P]], base=0, channel_multiplier=0, allow_small_or_imprecise_dtypes=True).then_inc(consts, 1)
            pool.iota(iota_we[:, :], pattern=[[1, P]], base=0, channel_multiplier=0, allow_small_or_imprecise_dtypes=True).then_inc(consts, 1)
            pool.iota(iota_p[:, :], pattern=[[0, 1]], base=0, channel_multiplier=1, allow_small_or_imprecise_dtypes=True).then_inc(consts, 1)
            pool.iota(penalty, pattern=[[1, CH]], base=0, channel_multiplier=0, allow_small_or_imprecise_dtypes=True).then_inc(consts, 1)
            pool.iota(window_node[:, :], pattern=[[NB, GROUPS + 1]], base=0, channel_multiplier=WN, allow_small_or_imprecise_dtypes=True).then_inc(consts, 1)

            def pass_waits():
                pool.sem_inc(passed, 1)

            def gather(slot, columns, copied, copied_value, done):
                pool.tensor_copy(src_idx[:, slot, :], columns).then_inc(copied, 1)
                pool.wait_ge(copied, copied_value)
                pass_waits()
                for j in range(J):
                    pool.indirect_dma_start(out=gathered[:, slot, j, :], out_offset=None, in_=x[:, :],
                                            in_offset=bass.IndirectOffsetOnAxis(ap=src_idx[:, slot, j:j + 1], axis=0)).then_inc(done, 16)

            def gather_chunk(m, n):
                slot = n % GATHER_SLOTS
                if n >= GATHER_SLOTS:
                    at_least(pool, chunk_done, m * PER_ROUND + A_POS[n - GATHER_SLOTS] + 1)
                else:
                    at_least(pool, chunk_done, (m - 1) * PER_ROUND + A_POS[A_ROUND + n - GATHER_SLOTS] + 1)
                pass_waits()
                gather(slot, src_col[:, bass.ds(m * A_ROUND + n, 1), :].rearrange("p a j -> p (a j)"), idx_copied,
                       m * A_ROUND + n + 1, x_in[slot])

            def search_row(job, group):
                at_least(pool, row_counted, job)
                pass_waits()
                pool.tensor_copy(row_idx[:, :], row_start_int[:, bass.ds(group, 1)]).then_inc(row_idx_set, 1)
                pool.wait_ge(row_idx_set, job + 1)
                pass_waits()
                pool.indirect_dma_start(out=rows[:, :], out_offset=None, in_=dst.rearrange("(r e) -> r e", e=ROW),
                                        in_offset=bass.IndirectOffsetOnAxis(ap=row_idx[:, 0:1], axis=1)).then_inc(row_in, 16)

            def load_windows(kind, number, arrays):
                pool.wait_ge(start_ready[kind], number + 1)
                pass_waits()
                for to, array in arrays:
                    pool.indirect_dma_start(out=to[:, :], out_offset=None, in_=array.rearrange("(r e) -> r e", e=WE),
                                            in_offset=bass.IndirectOffsetOnAxis(ap=start_int[kind][:, 0:1], axis=1)).then_inc(win_in[kind], 16)

            def step(m, half, odd, last):
                job = rows_before(half, odd)
                for s in range(SEGS):
                    if s < A_ROUND and not (isinstance(m, int) and m == 0 and s < GATHER_SLOTS):
                        if isinstance(m, int) and m == 0 and s == GATHER_SLOTS:
                            pool.wait_ge(src_in, 16)
                        gather_chunk(m, s)
                    if s == 0 and not last:
                        load_windows(0, m + 1, ((win_dst[0], dst), (win_src, src)))
                    if s == 1 and not odd and not last:
                        search_row(job, half)
                    if s == 2 and not last:
                        search_row(job + (0 if odd else 1), m + (G0 + 2))
                    if s == 4 and not odd and not last:
                        load_windows(1, half, ((win_dst[1], dst),))

            pool.wait_ge(src_first_in, 16)
            gather_chunk(0, 0)
            pool.wait_ge(offsets_ready, 1)
            search_row(0, G0)
            gather_chunk(0, 1)
            search_row(1, G0 + 1)
            load_windows(0, 0, ((win_dst[0], dst), (win_src, src)))
            in_turn(pool, ROUNDS, step)

            pool.wait_ge(flag_ready, 1)
            flag = pool.value_load(flag_int[0:1, 0:1], min_val=0, max_val=1)
            with pool.If(flag > 0):
                with pool.Fori(0, NCH) as c:
                    pool.wait_ge(fb_chunk_done, c + 1)
                    pool.wait_ge(fb_col_in, (c + 1) * 32)
                    pass_waits()
                    gather(0, fb_src_int, idx_copied, c + (CA + 1), fb_x_in)

        @block.tensor
        def _(pe):
            pe.wait_ge(firsts_ready, 1)
            pe.matmul(count_ps[2][:, 0:NROW], ones[0:1, :], scratch[0:1, :], start=True, stop=True).then_inc(firsts_spread, 1)
            pe.wait_ge(ident_ready, 2)
            pe.wait_ge(rel_nat_ready, 1)
            for t, n in ((0, P), (1, T1)):
                turned = count_ps[t][:, :].bitcast(BF16).rearrange("p (j c) -> p j c", j=J)
                for j in range(J):
                    mm = pe.transpose(turned[:, j, 0:n], rel_nat[0:n, t, j:CH:J], ident_bf[0:n, 0:n])
            mm.then_inc(rel_turned, 1)

            def prepare_weights():
                pe.wait_ge(small_in, 96)
                pe.transpose(turn_ps[:, 0:D], weights[:, 2, :], ident[:, :]).then_inc(wm_turned, 1)
                pe.wait_ge(wm_ready, 1)
                for k in range(2):
                    pe.matmul(turn_ps[:, k * D:(k + 1) * D], weights[:, k, :], wm_t[:, :], start=True, stop=True)
                pe.matmul(turn_ps[0:PB, 2 * D:3 * D], bias_rep[:, 0:PB], wm_t[:, :], start=True, stop=False)
                pe.matmul(turn_ps[0:PB, 2 * D:3 * D], ones[0:1, 0:PB], bias_m[:, :], start=False, stop=True).then_inc(weights_mm, 1)

            prepare_weights()

            def chunk_matmuls(bank, kinds, hot):
                for kind, rows_of in kinds:
                    for j in range(J):
                        mm = pe.matmul(bank[:, kind * W:(kind + 1) * W], rows_of[:, j, :], hot[:, j, :], start=(j == 0), stop=(j == J - 1))
                return mm

            def chunk(m, kind, n, pos):
                t = m * PER_ROUND + pos
                k = pos % EDGE_SLOTS
                pe.wait_ge(onehot_ready, t + 1)
                at_least(pe, chunk_added, t - CHUNK_BANKS + 1)
                pe.wait_ge(edge_in[k], (m * (PER_ROUND // EDGE_SLOTS) + (pos // EDGE_SLOTS + 1)) * 16)
                kinds = [(1, edges[:, k, :, :])]
                if kind == "A":
                    slot = n % GATHER_SLOTS
                    pe.wait_ge(x_in[slot], (m * (A_ROUND // GATHER_SLOTS) + (n // GATHER_SLOTS + 1)) * (16 * J))
                    kinds.append((0, gathered[:, slot, :, :]))
                chunk_matmuls(chunk_ps[pos % CHUNK_BANKS], kinds, onehot[:, pos % ONEHOT_SLOTS, :, :]).then_inc(chunk_done, 1)

            pe.wait_ge(prologue_done, 1)

            def turn_keys(m):
                pe.wait_ge(keys_ready, m + 1)
                at_least(pe, keys_spread, m)
                turned = turn_ps[:, :].bitcast(BF16)
                pe.transpose(turned[0:WE, 0:PB], row_bf[:, :], ident_bf[0:PB, 0:PB])
                pe.transpose(turned[0:WE, P:P + PB], key_bf[:, :], ident_bf[0:PB, 0:PB]).then_inc(keys_turned, 1)

            def count_batch(m, odd, s):
                pe.wait_ge(hots_ready, m * SEGS + (s + 1))
                slot = (SEGS * odd + s) % 2
                for f in range(FILLS):
                    fill = s * FILLS + f
                    bank = fill % M_BANKS
                    if fill >= M_BANKS:
                        pe.wait_ge(bank_moved, m * (SEGS * FILLS) + (fill - M_BANKS + 1))
                    else:
                        before = max(q for q in range(SEGS * FILLS) if q % M_BANKS == bank)
                        at_least(pe, bank_moved, (m - 1) * (SEGS * FILLS) + (before + 1))
                    for w in range(FILL):
                        win = f * FILL + w
                        mm = pe.matmul(count_ps[bank][:, w * KEYS:(w + 1) * KEYS], row_hot[0:WE, slot, win, :], key_hot[0:WE, slot, win, 0:KEYS],
                                       start=True, stop=True)
                    mm.then_inc(bank_filled, 1)

            def apply_x(g, odd, s):
                if s == 0:
                    pe.wait_ge(bank_moved, (g + 1) * (SEGS * FILLS))
                    at_least(pe, x_added, g)
                for b in range(BLOCK_CUTS[s], BLOCK_CUTS[s + 1]):
                    for part in range(3):
                        mm = pe.matmul(x_ps[:, 0:NB], x_parts[:, part, b, :], counts[odd][:, b, :],
                                       start=(b == 0 and part == 0), stop=(b == XB - 1 and part == 2))
                if s == SEGS - 1:
                    mm.then_inc(x_mm, 1)

            def step(m, half, odd, last):
                first = isinstance(m, int) and m == 0
                for s, seg in enumerate(chunks_of(last)):
                    for kind, n, pos in seg:
                        chunk(m, kind, n, pos)
                        if first and pos == CHUNK_BANKS - 1:
                            turn_keys(0)
                    count_batch(m, odd, s)
                    if isinstance(m, int) and m == 1 and s == 0:
                        pe.wait_ge(x_lo, XB // SPLIT_BLOCKS)
                    if not first:
                        apply_x(m - 1, 1 - odd, s)
                    if s == 2 and not last:
                        turn_keys(m + 1)

            in_turn(pe, ROUNDS, step)
            for s in range(SEGS):
                apply_x(ROUNDS - 1, 0, s)

            pe.wait_ge(caps_ready, 1)
            sums_of = chunk_ps[0]
            pe.wait_ge(chunk_added, NCH)
            pe.matmul(sums_of[0:1, 0:2], ones[:, 0:1], captured[:, 0:2], start=True, stop=True)
            pe.matmul(sums_of[0:1, 2:3], ones[0:CA, 0:1], captured[0:CA, 0:1], start=True, stop=True)
            pe.matmul(sums_of[0:1, 3:3 + ROUNDS], ones[0:PB, 0:1], captured[0:PB, 2:2 + ROUNDS], start=True, stop=True)
            pe.matmul(sums_of[0:1, 64:64 + WN * GROUPS], ones[0:PB, 0:1], degree[:, :], start=True, stop=True).then_inc(caps_summed, 1)

            pe.wait_ge(flag_ready, 1)
            flag = pe.value_load(flag_int[0:1, 0:1], min_val=0, max_val=1)
            with pe.If(flag > 0):
                with pe.Fori(0, NCH) as c:
                    with pe.Fori(0, WINDOWS) as w:
                        pe.wait_ge(fb_edge_in, (c + 1) * 16)
                        pe.wait_ge(fb_x_in, (c + 1) * (16 * J))
                        pe.wait_ge(fb_onehot, c * WINDOWS + w + 1)
                        chunk_matmuls(chunk_ps[0], [(1, edges[:, 0, :, :]), (0, gathered[:, 0, :, :])], onehot[:, 0, :, :]).then_inc(fb_mm, 1)

            def turn_applied(g, odd):
                pe.wait_ge(applied_moved, g + 1)
                at_least(pe, resid_ready, g * WN)
                for h in range(WN):
                    mm = pe.transpose(count_ps[2 + odd][0:PB, h * D:(h + 1) * D], applied[odd][:, h:NB:WN], ident[:, :])
                mm.then_inc(applied_turned, 1)

            def last_step(g, half, odd, last):
                at_least(pe, applied_moved, g - 1)
                for k in range(2):
                    mm = pe.matmul(count_ps[odd][:, 0:NB], w_both[:, k, :], sums[:, k, bass.ds(g * NB, NB)], start=(k == 0), stop=(k == 1))
                mm.then_inc(applied_mm, 1)
                if not (isinstance(g, int) and g == 0):
                    turn_applied(g - 1, 1 - odd)
            pe.wait_ge(sums_ready, 1)
            in_turn(pe, GROUPS, last_step)
            turn_applied(GROUPS - 1, 0)

        @block.vector
        def _(dve):
            steps = [0]

            def link(ins):
                steps[0] += 1
                ins.then_inc(dve_chain, 1)
                dve.wait_ge(dve_chain, steps[0])

            dve.memset(ones[:, :], 1.0)
            dve.memset(captured[:, :], 0.0)
            dve.memset(sums[:, :, :], 0.0)
            link(dve.memset(x_raw[:, (XB - 1) * D:XB * D], 0.0))
            dve.sem_inc(x_zeroed, 1)
            dve.wait_ge(firsts_in, 48)
            link(dve.tensor_copy(scratch[0:1, :], firsts_int[:, :]))
            dve.sem_inc(firsts_ready, 1)
            dve.tensor_scalar(base_int[:, :], chunk_firsts, float(NP - W), 0.0, ALU.min, ALU.max).then_inc(dve_chain, 1)
            steps[0] += 1
            dve.wait_ge(consts, 5)
            dve.tensor_scalar(ident[:, :], iota_we[:, :], iota_p[:, 0:1], None, ALU.is_equal).then_inc(ident_ready, 1)
            dve.tensor_scalar(ident_bf[:, :], iota_we[:, :], iota_p[:, 0:1], None, ALU.is_equal).then_inc(ident_ready, 1)
            dve.wait_ge(dst_in, 96)
            dve.tensor_scalar(is_last[:, :], iota_p[:, :], float(T1 - 1), 1.0e5, ALU.is_equal, ALU.mult)
            link(dve.tensor_scalar(first_col[:, 0:1], first_col_int[:, 0:1], float(NP - W), None, ALU.min))
            link(dve.tensor_scalar(first_col[0:T1, 1:2], first_col_int[0:T1, 1:2], float(NP - W), None, ALU.min))
            link(dve.tensor_scalar(penalty[0:T1, :], penalty[0:T1, :], float(REPEATED), is_last[0:T1, 0:1], ALU.is_lt, ALU.mult))
            dve.tensor_scalar(rel_nat[:, 0, :], dst_nat[:, 0, :], first_col[:, 0:1], None, ALU.subtract)
            link(dve.scalar_tensor_tensor(rel_nat[0:T1, 1, :], dst_nat[0:T1, 1, :], first_col[0:T1, 1:2], penalty[0:T1, :], ALU.subtract, ALU.subtract))
            dve.sem_inc(rel_nat_ready, 1)

            dve.wait_ge(firsts_spread, 1)
            link(dve.tensor_copy(firsts, count_ps[2][:, 0:NROW]))
            samples = penalty[0:PB, 0:NROW]
            for g in range(GROUPS + 1):
                link(dve.tensor_scalar(samples, firsts[0:PB, :], window_node[:, g:g + 1], None, ALU.is_lt, ALU.add,
                                       accum_out=row_count[:, g:g + 1]))
            link(dve.tensor_scalar(row_start[:, :], row_count[:, :], float(ROW), -float(ROW), ALU.mult, ALU.add))
            link(dve.tensor_scalar(row_start[:, :], row_start[:, :], 0.0, float(E - ROW), ALU.max, ALU.min))
            link(dve.tensor_copy(row_start_int[:, :], row_start[:, :]))
            dve.tensor_scalar(node_half[:, :], window_node[:, :], -0.5, None, ALU.add)
            link(dve.tensor_scalar(row_middle[:, :], row_start[:, :], float(ROW // 2), None, ALU.add))
            dve.sem_inc(offsets_ready, 1)

            dve.wait_ge(rel_turned, 1)
            for t, n in ((0, P), (1, T1)):
                turned = count_ps[t][:, :].bitcast(BF16).rearrange("p (j c) -> p c j", j=J)
                link(dve.tensor_copy(rel_col[:, t * P:t * P + n, :], turned[:, 0:n, :]))

            inside = penalty.bitcast(BF16)[:, 0:CH]
            for t, n in ((0, P), (1, T1)):
                link(dve.tensor_scalar(inside[0:n, :], rel_nat[0:n, t, :], 0.0, None, ALU.is_ge))
                link(dve.scalar_tensor_tensor(inside[0:n, :], rel_nat[0:n, t, :], float(W), inside[0:n, :], ALU.is_lt, ALU.mult,
                                              accum_out=captured[0:n, t:t + 1]))
            dve.wait_ge(small_in, 96)
            link(dve.tensor_scalar(bias_rep[:, :], ones[:, :], bias_col[:, 0:1], bias_col[:, 1:2], ALU.mult, ALU.add))
            dve.wait_ge(wm_turned, 1)
            link(dve.tensor_copy(wm_t[:, :], turn_ps[:, 0:D]))
            dve.sem_inc(wm_ready, 1)
            dve.wait_ge(weights_mm, 1)
            dve.tensor_copy(w_both[:, :, :], turn_ps[:, 0:2 * D].rearrange("p (k d) -> p k d", k=2))
            link(dve.tensor_copy(bias_row[:, :], turn_ps[0:PB, 2 * D:3 * D]))
            dve.sem_inc(prologue_done, 1)

            def find_start(job, kind, group):
                dve.wait_ge(row_counted, job + 1)
                dve.scalar_tensor_tensor(start_tmp[:, :], sign_sum[:, :], 0.5, row_middle[:, bass.ds(group, 1)], ALU.mult, ALU.add).then_inc(start_step, 1)
                dve.wait_ge(start_step, job * 2 + 1)
                dve.tensor_scalar(start[kind][:, :], start_tmp[:, :], float(E - WE), 0.0, ALU.min, ALU.max).then_inc(start_step, 1)
                dve.wait_ge(start_step, job * 2 + 2)
                dve.tensor_copy(start_int[kind][:, :], start[kind][:, :]).then_inc(start_ready[kind], 1)

            def count_degree(kind, group, unit):
                for h in range(WN):
                    dve.tensor_scalar(held[:, h, :], rel_key[:, :], float(unit * h), None, ALU.is_equal, ALU.add,
                                      accum_out=degree[:, bass.ds(group * WN + h, 1)]).then_inc(degree_step, 1)

            def make_keys(m, jobs):
                group = m + G0
                dve.wait_ge(win_in[0], (m + 1) * 32)
                at_least(dve, keys_turned, m)
                dve.tensor_scalar(src_block[:, :], win_src[:, :], 7, None, ALU.logical_shift_right).then_inc(key_step, 1)
                dve.tensor_scalar(src_row[:, :], win_src[:, :], P - 1, None, ALU.bitwise_and).then_inc(key_step, 1)
                at_least(dve, degree_step, jobs * WN)
                dve.tensor_scalar(rel_key[:, :], win_dst[0][:, :], window_node[:, bass.ds(group, 1)], float(XB), ALU.subtract, ALU.mult).then_inc(key_step, 1)
                dve.tensor_scalar(early_edge[:, :], iota_we[0:PB, 0:WE], start[0][:, 0:1], float(CA * CH), ALU.add, ALU.is_lt).then_inc(key_step, 1)
                dve.wait_ge(key_step, m * 6 + 4)
                dve.tensor_tensor(key[:, :], rel_key[:, :], src_block[:, :], ALU.add).then_inc(key_step, 1)
                dve.tensor_copy(row_bf[:, :], src_row[:, :]).then_inc(key_step, 1)
                dve.wait_ge(key_step, m * 6 + 6)
                dve.scalar_tensor_tensor(key_bf[:, :], early_edge[:, :], 1024.0, key[:, :], ALU.mult, ALU.add).then_inc(keys_ready, 1)
                count_degree(0, group, XB)
                dve.wait_ge(degree_step, jobs * WN + WN)
                dve.wait_ge(keys_ready, m + 1)
                dve.tensor_scalar(held[:, WN, :], key_bf[:, :], 0.0, None, ALU.is_ge).then_inc(keys_used, 1)
                dve.wait_ge(keys_used, m * 2 + 1)
                dve.scalar_tensor_tensor(held[:, WN, :], key_bf[:, :], float(KEYS), held[:, WN, :], ALU.is_lt, ALU.mult,
                                         accum_out=captured[0:PB, bass.ds(m + 2, 1)]).then_inc(keys_used, 1)
                dve.wait_ge(keys_used, m * 2 + 2)

            def only_degrees(k, jobs):
                dve.wait_ge(win_in[1], (k + 1) * 16)
                at_least(dve, degree_step, jobs * WN)
                dve.tensor_scalar(rel_key[:, :], win_dst[1][:, :], window_node[:, bass.ds(k, 1)], None, ALU.subtract).then_inc(only_step, 1)
                dve.wait_ge(only_step, k + 1)
                count_degree(1, k, 1)

            def degrees_before(half, odd):
                return half * 3 + (3 if odd else 1)

            def make_hots(m, odd, s):
                slot = (SEGS * odd + s) % 2
                if s == 0:
                    dve.wait_ge(keys_spread, m + 1)
                at_least(dve, bank_filled, m * (SEGS * FILLS) + (s - 1) * FILLS)
                for hot, four, width in ((row_hot, row4, P), (key_hot, key4, KPAD)):
                    shape = [WE, BATCH, width // 4, 4]
                    ins = dve.tensor_tensor(hot[0:WE, slot, :, :].rearrange("p w (a b) -> p w a b", b=4),
                                            iota_bf[0:WE, 0:width].rearrange("p (c a b) -> p c a b", c=1, b=4).to_broadcast(shape),
                                            four[0:WE, odd, s * BATCH:(s + 1) * BATCH, :].rearrange("p w (a b) -> p w a b", a=1).to_broadcast(shape),
                                            ALU.is_equal)
                ins.then_inc(hots_ready, 1)

            def make_onehot(m, kind, n, pos):
                t = m * PER_ROUND + pos
                at_least(dve, chunk_done, t - ONEHOT_SLOTS + 1)
                rel = rel_col[:, bass.ds(chunk_id(m, kind, n), 1), :]
                dve.tensor_tensor(onehot[:, pos % ONEHOT_SLOTS, :, :], iota_bf[:, 0:W].rearrange("p (a w) -> p a w", a=1).to_broadcast([P, J, W]),
                                  rel.rearrange("p a j -> p j a").to_broadcast([P, J, W]), ALU.is_equal).then_inc(onehot_ready, 1)

            def add_chunk(m, kind, n, pos, groups_added):
                t = m * PER_ROUND + pos
                at = dve.value_load(base_int[0:1, bass.ds(chunk_id(m, kind, n), 1)], min_val=0, max_val=NP - W)
                at_least(dve, chunk_added, t)
                at_least(dve, x_added, groups_added)
                dve.wait_ge(chunk_done, t + 1)
                k0, kn = (0, 2) if kind == "A" else (1, 1)
                to = sums[:, k0:2, bass.ds(at, W)]
                dve.tensor_tensor(to, to, chunk_ps[pos % CHUNK_BANKS][:, k0 * W:2 * W].rearrange("p (k w) -> p k w", k=kn), ALU.add).then_inc(chunk_added, 1)

            def add_group(g, chunks):
                at_least(dve, chunk_added, chunks)
                dve.wait_ge(x_mm, g + 1)
                to = sums[:, 0, bass.ds((g + G0) * NB, NB)]
                dve.tensor_tensor(to, to, x_ps[:, 0:NB], ALU.add).then_inc(x_added, 1)

            def split_rest(to, part, seen, signal):
                wide = SPLIT_BLOCKS * D
                for k in range(XB // SPLIT_BLOCKS):
                    dve.wait_ge(seen, k + 1)
                    dve.tensor_tensor(to(k), x_raw[:, k * wide:(k + 1) * wide],
                                      x_parts[:, part, k * SPLIT_BLOCKS:(k + 1) * SPLIT_BLOCKS, :].rearrange("p b d -> p (b d)"),
                                      ALU.subtract).then_inc(signal, 1)

            def step(m, half, odd, last):
                first = isinstance(m, int) and m == 0
                second = isinstance(m, int) and m == 1
                groups_added = m - 1 if not (first or second) else 0
                for s, seg in enumerate(chunks_of(last)):
                    if s == 0 and not first and not second:
                        add_group(m - 2, m * PER_ROUND - 1)
                    for kind, n, pos in seg:
                        ahead = after(m, last, pos, ONEHOT_SLOTS - 1)
                        if ahead is not None:
                            am, akind, an = ahead
                            flat = pos + ONEHOT_SLOTS - 1
                            over = flat >= PER_ROUND and not last
                            make_onehot(am, akind, an, flat - PER_ROUND if over else flat)
                        if pos > 0:
                            back = [c for sg in chunks_of(last) for c in sg][pos - 1]
                            add_chunk(m, back[0], back[1], back[2], groups_added)
                        elif not first:
                            back = [c for sg in chunks_of(False) for c in sg][-1]
                            add_chunk(m - 1, back[0], back[1], back[2], groups_added)
                    if s < SEGS - 1:
                        make_hots(m, odd, s + 1)
                    elif not last:
                        make_hots(m + 1, 1 - odd, 0)
                    if s == 0 and odd:
                        only_degrees(half, degrees_before(half, 1) - 1)
                    if s == 1 and not last:
                        make_keys(m + 1, degrees_before(half, odd))
                    if s == 2 and not odd and not last:
                        find_start(rows_before(half, 0), 1, half)
                    if s == 3 and not last:
                        find_start(rows_before(half, odd) + (0 if odd else 1), 0, m + (G0 + 2))
                    if first and s == 0:
                        split_rest(lambda k: x_raw[:, k * SPLIT_BLOCKS * D:(k + 1) * SPLIT_BLOCKS * D], 0, x_hi, x_rest)
                    if first and s == 2:
                        split_rest(lambda k: x_parts[:, 2, k * SPLIT_BLOCKS:(k + 1) * SPLIT_BLOCKS, :].rearrange("p b d -> p (b d)"), 1, x_mid, x_lo)

            make_onehot(0, "A", 0, 0)
            make_onehot(0, "B", 0, 1)
            find_start(0, 0, G0)
            make_keys(0, 0)
            find_start(1, 0, G0 + 1)
            make_hots(0, 0, 0)
            in_turn(dve, ROUNDS, step)
            flat = [c for sg in chunks_of(True) for c in sg]
            add_chunk(ROUNDS - 1, *flat[-1], ROUNDS - 2)
            dve.wait_ge(degree_step, GROUPS * WN)
            dve.wait_ge(keys_used, ROUNDS * 2)
            dve.sem_inc(caps_ready, 1)
            add_group(ROUNDS - 2, NCH)
            dve.wait_ge(x_added, ROUNDS - 1)
            add_group(ROUNDS - 1, NCH)
            dve.wait_ge(caps_summed, 1)
            dve.tensor_reduce(totals[:, 0:1], chunk_ps[0][0:1, 0:2], AX.X, ALU.add)
            dve.tensor_reduce(totals[:, 1:2], chunk_ps[0][0:1, 2:3 + ROUNDS], AX.X, ALU.add)
            link(dve.tensor_reduce(totals[:, 2:3], chunk_ps[0][0:1, 64:64 + WN * GROUPS], AX.X, ALU.add))
            link(dve.tensor_scalar(totals[:, 0:3], totals[:, 0:3], float(E), None, ALU.not_equal))
            link(dve.tensor_reduce(totals[:, 3:4], totals[:, 0:3], AX.X, ALU.max))
            dve.tensor_copy(flag_int[:, :], totals[:, 3:4]).then_inc(flag_ready, 1)
            dve.wait_ge(flag_ready, 1)
            dve.wait_ge(x_added, ROUNDS)
            flag = dve.value_load(flag_int[0:1, 0:1], min_val=0, max_val=1)
            with dve.If(flag > 0):
                dve.memset(sums[:, :, :], 0.0).then_inc(fb_chain, 1)
                dve.memset(degree[:, :], 0.0).then_inc(fb_chain, 1)
                dve.wait_ge(fb_chain, 2)
                dve.sem_inc(fb_chunk_done, 1)

                def fb_chunk(c, last):
                    dve.wait_ge(fb_col_in, (c + 1) * 32)
                    dve.tensor_copy(fb_rel, fb_dst_int).then_inc(fb_moved, 1)
                    if last:
                        dve.wait_ge(fb_moved, c * (WINDOWS + 1) + 1)
                        dve.tensor_scalar(fb_pos, iota_p[:, 0:1].to_broadcast([P, J]), float(J), None, ALU.mult).then_inc(fb_chain, 1)
                        dve.wait_ge(fb_chain, 3)
                        dve.tensor_tensor(fb_pos, fb_pos, iota_we[:, 0:J], ALU.add).then_inc(fb_chain, 1)
                        dve.wait_ge(fb_chain, 4)
                        dve.tensor_scalar(fb_pos, fb_pos, float(REPEATED), -1.0e5, ALU.is_lt, ALU.mult).then_inc(fb_chain, 1)
                        dve.wait_ge(fb_chain, 5)
                        dve.tensor_tensor(fb_rel, fb_rel, fb_pos, ALU.add).then_inc(fb_chain, 1)
                        dve.wait_ge(fb_chain, 6)
                    with dve.Fori(0, WINDOWS) as w:
                        n = c * WINDOWS + w
                        dve.wait_ge(fb_moved, n + c + 1)
                        dve.tensor_tensor(onehot[:, 0, :, :], iota_bf[:, 0:W].rearrange("p (a w) -> p a w", a=1).to_broadcast([P, J, W]),
                                          fb_rel.rearrange("p (j a) -> p j a", a=1).to_broadcast([P, J, W]), ALU.is_equal).then_inc(fb_onehot, 1)
                        dve.wait_ge(fb_onehot, n + 1)
                        dve.tensor_scalar(fb_rel, fb_rel, -float(W), None, ALU.add).then_inc(fb_moved, 1)
                        dve.wait_ge(fb_mm, n + 1)
                        to = sums[:, :, bass.ds(w * W, W)]
                        dve.tensor_tensor(to, to, chunk_ps[0][:, 0:2 * W].rearrange("p (k w) -> p k w", k=2), ALU.add).then_inc(fb_added, 1)
                        dve.wait_ge(fb_added, n + 1)
                    e0 = REPEATED if last else 0
                    dve.wait_ge(fb_row_in, (c + 1) * 16)
                    dve.tensor_copy(fb_row, fb_row_int).then_inc(fb_counted, 1)
                    with dve.Fori(0, WN * GROUPS) as k:
                        n = c * (2 * WN * GROUPS + 1) + k * 2 + 1
                        dve.wait_ge(fb_counted, n)
                        dve.tensor_scalar(fb_equal[:, e0:CH], fb_row[:, e0:CH], fb_node[:, bass.ds(k, 1)], None, ALU.is_equal, ALU.add,
                                          accum_out=start_tmp[:, :]).then_inc(fb_counted, 1)
                        dve.wait_ge(fb_counted, n + 1)
                        dve.tensor_tensor(degree[:, bass.ds(k, 1)], degree[:, bass.ds(k, 1)], start_tmp[:, :], ALU.add).then_inc(fb_counted, 1)
                    dve.wait_ge(fb_counted, (c + 1) * (2 * WN * GROUPS + 1))
                    dve.sem_inc(fb_chunk_done, 1)

                for h in range(WN):
                    dve.tensor_scalar(fb_node.rearrange("p (g h) -> p g h", h=WN)[:, :, h], window_node[:, 0:GROUPS], float(h), None, ALU.add).then_inc(fb_chain2, 1)
                dve.wait_ge(fb_chain2, WN)
                with dve.Fori(0, NFULL) as c:
                    fb_chunk(c, False)
                fb_chunk(NFULL, True)

            dve.tensor_scalar(has_edge[:, :], degree[:, :], 1.0, None, ALU.min).then_inc(tail_step, 1)
            dve.tensor_scalar(recip[:, :], degree[:, :], 1.0, None, ALU.max).then_inc(tail_step, 1)
            dve.wait_ge(tail_step, 2)
            dve.reciprocal(recip[:, :], recip[:, :]).then_inc(tail_step, 1)
            dve.sem_inc(sums_ready, 1)
            dve.wait_ge(tail_step, 3)
            dve.wait_ge(resid_in, 16)
            with dve.Fori(0, WN * GROUPS) as k:
                row = resid[:, bass.ds(k, 1), :].rearrange("p a d -> p (a d)")
                dve.scalar_tensor_tensor(row, bias_row[:, :], has_edge[:, bass.ds(k, 1)], row, ALU.mult, ALU.add).then_inc(resid_biased, 1)
            dve.wait_ge(resid_biased, WN * GROUPS)
            dve.sem_inc(resid_ready, WN)

            def last_step(g, half, odd, last):
                dve.wait_ge(applied_turned, g + 1)
                for h in range(WN):
                    k = g * WN + h
                    row = resid[:, bass.ds(k, 1), :].rearrange("p a d -> p (a d)")
                    dve.scalar_tensor_tensor(row, count_ps[2 + odd][0:PB, h * D:(h + 1) * D], recip[:, bass.ds(k, 1)], row, ALU.mult, ALU.add).then_inc(resid_ready, 1)
                dve.wait_ge(resid_ready, (g + 2) * WN)
                for h in range(WN):
                    k = g * WN + h
                    dve.bn_stats(stats[:, bass.ds(k, 1), :].rearrange("p a s -> p (a s)"),
                                 resid[:, bass.ds(k, 1), :].rearrange("p a d -> p (a d)")).then_inc(stats_done, 1)

            in_turn(dve, GROUPS, last_step)
            dve.wait_ge(stats_done, WN * GROUPS)
            dve.tensor_tensor(mean[:, :], stats[:, :, 1], stats[:, :, 4], ALU.add)
            dve.tensor_tensor(half_gap[:, :], stats[:, :, 1], stats[:, :, 4], ALU.subtract)
            link(dve.tensor_tensor(var_eps[:, :], stats[:, :, 2], stats[:, :, 5], ALU.add))
            dve.tensor_scalar(mean[:, :], mean[:, :], 0.5, None, ALU.mult)
            dve.tensor_scalar(var_eps[:, :], var_eps[:, :], 1.0 / D, EPS, ALU.mult, ALU.add)
            link(dve.tensor_scalar(half_gap[:, :], half_gap[:, :], 0.5, None, ALU.mult))
            link(dve.tensor_tensor(half_gap[:, :], half_gap[:, :], half_gap[:, :], ALU.mult))
            dve.tensor_tensor(var_eps[:, :], var_eps[:, :], half_gap[:, :], ALU.add).then_inc(var_ready, 1)
            dve.wait_ge(std_ready, 1)
            link(dve.reciprocal(rstd[:, :], stddev[:, :]))
            with dve.Fori(0, WN * GROUPS) as k:
                row = resid[:, bass.ds(k, 1), :].rearrange("p a d -> p (a d)")
                dve.tensor_scalar(row, row, mean[:, bass.ds(k, 1)], rstd[:, bass.ds(k, 1)], ALU.subtract, ALU.mult).then_inc(y_ready, 1)

        @block.scalar
        def _(act):
            def round_part(part, seen, signal):
                wide = SPLIT_BLOCKS * D
                for k in range(XB // SPLIT_BLOCKS):
                    if seen is not None:
                        act.wait_ge(seen, k + 1)
                    act.copy(x_parts[:, part, k * SPLIT_BLOCKS:(k + 1) * SPLIT_BLOCKS, :].rearrange("p b d -> p (b d)"),
                             x_raw[:, k * wide:(k + 1) * wide]).then_inc(signal, 1)

            def count_row(job, group):
                act.wait_ge(row_in, (job + 1) * 16)
                at_least(act, start_step, job * 2)
                act.activation(row_signs[:, :], rows[:, :], ACT.Sign, bias=node_half[:, bass.ds(group, 1)], scale=-1.0,
                               accum_out=sign_sum[:, :]).then_inc(row_counted, 1)

            def spread_keys(m, odd):
                act.wait_ge(keys_turned, m + 1)
                turned = turn_ps[:, :].bitcast(BF16)
                at_least(act, bank_filled, (m - 1) * (SEGS * FILLS))
                for four, at in ((row4, 0), (key4, P)):
                    ins = act.copy(four[0:WE, odd, :, :], turned[0:WE, at:at + PB].rearrange("p (w a) -> p w a", a=1).to_broadcast([WE, PB, 4]))
                ins.then_inc(keys_spread, 1)

            def move_bank(m, odd, fill):
                act.wait_ge(bank_filled, m * (SEGS * FILLS) + (fill + 1))
                act.copy(counts[odd][:, :, fill * FILL * WN:(fill + 1) * FILL * WN],
                         count_ps[fill % M_BANKS][:, 0:FILL * KEYS].rearrange("p (n b) -> p b n", b=XB)).then_inc(bank_moved, 1)

            def step(m, half, odd, last):
                first = isinstance(m, int) and m == 0
                for s in range(SEGS):
                    if s == 0:
                        at_least(act, x_mm, m - 1)
                    if s == 1 and first:
                        round_part(1, x_rest, x_mid)
                    if s == 0 and isinstance(m, int) and m == 1:
                        act.wait_ge(x_lo, XB // SPLIT_BLOCKS)
                    if s == 2 and not odd and not last:
                        count_row(rows_before(half, 0), half)
                    if s == 3 and not last:
                        spread_keys(m + 1, 1 - odd)
                        count_row(rows_before(half, odd) + (0 if odd else 1), m + (G0 + 2))
                    for f in range(FILLS):
                        move_bank(m, odd, s * FILLS + f)

            act.wait_ge(offsets_ready, 1)
            count_row(0, G0)
            act.wait_ge(x_raw_in, 32)
            round_part(0, None, x_hi)
            count_row(1, G0 + 1)
            spread_keys(0, 0)
            act.wait_ge(prologue_done, 1)
            in_turn(act, ROUNDS, step)

            def last_step(g, half, odd, last):
                act.wait_ge(applied_mm, g + 1)
                at_least(act, applied_turned, g - 1)
                act.copy(applied[odd], count_ps[odd][:, 0:NB]).then_inc(applied_moved, 1)

            act.wait_ge(sums_ready, 1)
            in_turn(act, GROUPS, last_step)
            act.wait_ge(var_ready, 1)
            act.activation(stddev[:, :], var_eps[:, :], ACT.Sqrt).then_inc(std_ready, 1)
            with act.Fori(0, GROUPS) as g:
                act.wait_ge(y_ready, (g + 1) * WN)
                act.dma_start(out_pairs[g], resid[:, bass.ds(g * WN, WN), :]).then_inc(out_done, 16)
            act.wait_ge(out_done, GROUPS * 16)


_INS = ["x", "src", "dst", "edge_attr_128", "L0_gnn_W_node", "L0_gnn_b_node", "L0_gnn_W_edge", "L0_gnn_b_edge",
        "L0_gnn_W_msg", "L0_gnn_b_msg"]


def kernel(**inputs):
    import numpy as _np
    import concourse.bacc as _bacc
    from concourse import mybir as _mybir
    from concourse.bass_utils import run_bass_kernel_spmd as _run

    nc = _bacc.Bacc("TRN2", target_bir_lowering=False, num_devices=1)
    arrays, args = {}, []
    for name in _INS:
        a = _np.ascontiguousarray(inputs[name])
        arrays[f"in_{name}_dram"] = a
        args.append(nc.dram_tensor(f"in_{name}_dram", a.shape, _mybir.dt.from_np(a.dtype), kind="ExternalInput").ap())
    out = nc.dram_tensor("out_dram", inputs["x"].shape, _mybir.dt.float32, kind="ExternalOutput").ap()
    gnn_layer(nc, *args, out)
    r = _run(nc, [arrays], core_ids=[0])
    return r.results[0]["out_dram"]
```

```python
from contextlib import ExitStack

import concourse.bass as bass
from concourse import mybir

ALU = mybir.AluOpType
ACT = mybir.ActivationFunctionType
AX = mybir.AxisListType
F32 = mybir.dt.float32
BF16 = mybir.dt.bfloat16
I32 = mybir.dt.int32

P = 128
D = 128
EPS = 1e-5

CH = 1024
J = CH // P
W = 64

WN = 2
WE = 125
NB = 250
PB = NB // WN
BATCH = 25
SEGS = PB // BATCH
FILL = 5
FILLS = BATCH // FILL
ROW = 550

A_ROUND, B_ROUND = 4, 8
SEG_CHUNKS = [[("A", 0), ("B", 0), ("B", 1)], [("A", 1), ("B", 2), ("B", 3)], [("A", 2), ("B", 4), ("B", 5)],
              [("A", 3), ("B", 6)], [("B", 7)]]
PER_ROUND = A_ROUND + B_ROUND
EDGE_SLOTS = 3
ONEHOT_SLOTS = 3
GATHER_SLOTS = 2
CHUNK_BANKS = 2
M_BANKS = 4
SPAN = 5
ACT_SHARE = 2
SPLIT_BLOCKS = 7


def gnn_layer(nc, x, src, dst, edge_attr, w_node, b_node, w_edge, b_edge, w_msg, b_msg, out):
    N = x.shape[0]
    E = edge_attr.shape[0]
    NFULL = E // CH
    OWN = NFULL * CH
    REPEATED = CH - (E - OWN)
    NCH = NFULL + 1
    GROUPS = N // NB
    SPANS = GROUPS // SPAN
    ROUNDS = (2 * GROUPS + 1) // 3
    G0 = GROUPS - ROUNDS
    CA = A_ROUND * ROUNDS
    LAST_B = NCH - CA - B_ROUND * (ROUNDS - 1)
    PAIRS = (ROUNDS - 3) // 2
    XB = -(-N // P)
    KEYS = WN * XB
    KPAD = -(-KEYS // 4) * 4
    WINDOWS = -(-N // W)
    NP = WINDOWS * W
    NROW = E // ROW
    T1 = NCH - P
    assert N % NB == 0 and NB % WN == 0 and FILL * KEYS <= 512
    assert 1 <= LAST_B <= B_ROUND and G0 == 1 + PAIRS, (ROUNDS, G0, LAST_B)
    assert CA <= P and CA * CH * N >= (G0 * NB + 50) * E
    assert GROUPS % SPAN == 0
    assert E % ROW == 0 and E % WE == 0 and NROW <= 512 and WE <= P

    with ExitStack() as ctx:
        def sb(name, shape, dt=F32):
            return ctx.enter_context(nc.sbuf_tensor(name, shape, dt))

        def psum(name):
            return ctx.enter_context(nc.psum_tensor(name, [P, 512], F32))

        def sem(name):
            return ctx.enter_context(nc.semaphore(name))

        sums = sb("sums", [P, 2, NP])
        x_parts = sb("x_parts", [P, 3, XB, D], BF16)
        COUNTS = XB * NB
        region = sb("region", [P, COUNTS // 2 + max(COUNTS // 2, WN * GROUPS * D, XB * D)])
        degree = sb("degree", [PB, WN * GROUPS])
        captured = sb("captured", [P, 2 + ROUNDS])

        HALF = COUNTS // 2
        slot0, slot1 = region[:, 0:HALF], region[:, HALF:]
        counts = [region[:, k * HALF:(k + 1) * HALF].bitcast(BF16).rearrange("p (b n) -> p b n", b=XB) for k in range(2)]
        place = [0]

        def early(n, dt=F32):
            at = place[0]
            place[0] += n
            assert place[0] <= HALF
            return region[:, at:at + n].bitcast(dt) if dt != F32 else region[:, at:at + n]

        dst_nat = early(2 * CH, I32).rearrange("p (t e) -> p t e", t=2)
        rel_nat = early(CH, BF16).rearrange("p (t e) -> p t e", t=2)
        penalty = early(CH)
        firsts_int = early(NROW, I32)[0:1, :]
        chunk_firsts = early(NCH, I32)[0:1, :]
        weights = early(3 * D).rearrange("p (n d) -> p n d", n=3)
        wm_t = early(D)
        bias_rep = early(P)
        firsts = early(NROW)
        scratch = early(NROW)
        x_raw = slot1[:, 0:XB * D]
        resid = slot1[0:PB, 0:WN * GROUPS * D].rearrange("p (k d) -> p k d", d=D)

        edges = sb("edges", [P, EDGE_SLOTS, J, D])
        gathered = sb("gathered", [P, GATHER_SLOTS, J, D])
        onehot = sb("onehot", [P, ONEHOT_SLOTS, J, W])
        row_hot = sb("row_hot", [P, 2, BATCH, P], BF16)
        key_hot = sb("key_hot", [P, 2, BATCH, KPAD], BF16)
        row4 = sb("row4", [P, 2, PB, 4], BF16)
        key4 = sb("key4", [P, 2, PB, 4], BF16)
        rel_col = sb("rel_col", [P, NCH, J], BF16)
        src_col = sb("src_col", [P, CA, J], I32)
        src_idx = sb("src_idx", [P, GATHER_SLOTS, J], I32)
        base_int = sb("base_int", [1, NCH], I32)
        first_col_int = sb("first_col_int", [P, 2], I32)
        first_col = sb("first_col", [P, 2])
        is_last = sb("is_last", [P, 1])

        window_node = sb("window_node", [PB, GROUPS + 1])
        node_half = sb("node_half", [PB, GROUPS + 1])
        row_count = sb("row_count", [PB, GROUPS + 1])
        row_start = sb("row_start", [PB, GROUPS + 1])
        row_start_int = sb("row_start_int", [PB, GROUPS + 1], I32)
        row_middle = sb("row_middle", [PB, GROUPS + 1])
        row_idx = sb("row_idx", [PB, 1], I32)
        rows = sb("rows", [PB, ROW], I32)
        row_signs = sb("row_signs", [PB, ROW], BF16)
        sign_sum = sb("sign_sum", [PB, 1])
        start_tmp = sb("start_tmp", [PB, 1])
        start = [sb(f"start{k}", [PB, 1]) for k in range(2)]
        start_int = [sb(f"start_int{k}", [PB, 1], I32) for k in range(2)]
        win_dst = [sb(f"win_dst{k}", [PB, WE], I32) for k in range(2)]
        win_src = sb("win_src", [PB, WE], I32)
        src_block = sb("src_block", [PB, WE], I32)
        src_row = sb("src_row", [PB, WE], I32)
        rel_key = sb("rel_key", [PB, WE])
        early_edge = sb("early_edge", [PB, WE])
        key = sb("key", [PB, WE])
        key_bf = sb("key_bf", [PB, WE], BF16)
        row_bf = sb("row_bf", [PB, WE], BF16)
        held = sb("held", [PB, WN + 1, WE], BF16)

        iota_bf = sb("iota_bf", [P, P], BF16)
        iota_we = sb("iota_we", [P, P])
        iota_p = sb("iota_p", [P, 1])
        ident = sb("ident", [P, P])
        ident_bf = sb("ident_bf", [P, P], BF16)
        ones = sb("ones", [P, P])
        w_both = sb("w_both", [P, 2, D])
        bias_col = sb("bias_col", [P, 2])
        bias_m = sb("bias_m", [1, D])
        bias_row = sb("bias_row", [PB, D])
        totals = sb("totals", [1, 4])
        flag_int = sb("flag_int", [1, 1], I32)

        late_words = gathered[0:PB, 1, :, :].rearrange("p j d -> p (j d)")
        late_names = ("mean", "half_gap", "var_eps", "stddev", "rstd", "shift", "recip", "has_edge")
        mean, half_gap, var_eps, stddev, rstd, shift, recip, has_edge = (
            late_words[:, k * WN * GROUPS:(k + 1) * WN * GROUPS] for k in range(len(late_names)))
        stats = late_words[:, len(late_names) * WN * GROUPS:(len(late_names) + 6) * WN * GROUPS].rearrange("p (k s) -> p k s", s=6)
        applied = [edges[:, 0, :, :].rearrange("p j d -> p (j d)")[:, k * CH // 2:k * CH // 2 + NB] for k in range(2)]
        bias_rows = edges[0:PB, 1:3, :, :].rearrange("p s j d -> p (s j) d")[:, 0:SPAN * WN, :]

        fb_row_int = edges[0:PB, 1, :, :].rearrange("p j d -> p (j d)").bitcast(I32)
        fb_row = edges[0:PB, 2, :, :].rearrange("p j d -> p (j d)")
        fb_equal = gathered[0:PB, 1, :, :].rearrange("p j d -> p (j d)")
        fb_dst_int = src_col[:, 0, :]
        fb_src_int = src_col[:, 1, :]
        fb_rel = sb("fb_rel", [P, J])[:, :]
        fb_pos = sb("fb_pos", [P, J])[:, :]
        fb_node = sb("fb_node", [PB, WN * GROUPS])[:, :]

        chunk_ps = [psum(f"chunk_ps{k}") for k in range(CHUNK_BANKS)]
        count_ps = [psum(f"count_ps{k}") for k in range(M_BANKS)]
        x_ps = psum("x_ps")
        turn_ps = psum("turn_ps")

        firsts_in = sem("firsts_in")
        dst_in = sem("dst_in")
        src_first_in = sem("src_first_in")
        src_in = sem("src_in")
        x_raw_in = sem("x_raw_in")
        small_in = sem("small_in")
        consts = sem("consts")
        ident_ready = sem("ident_ready")
        firsts_ready = sem("firsts_ready")
        firsts_spread = sem("firsts_spread")
        rel_nat_ready = sem("rel_nat_ready")
        rel_turned = sem("rel_turned")
        wm_turned = sem("wm_turned")
        wm_ready = sem("wm_ready")
        weights_mm = sem("weights_mm")
        prologue_done = sem("prologue_done")
        offsets_ready = sem("offsets_ready")
        x_zeroed = sem("x_zeroed")
        sums_zeroed = sem("sums_zeroed")
        half_ready = sem("half_ready")
        firsts_copied = sem("firsts_copied")
        rows_before_ready = sem("rows_before_ready")
        x_hi = sem("x_hi")
        x_rest = sem("x_rest")
        x_mid = sem("x_mid")
        x_lo = sem("x_lo")
        dve_chain = sem("dve_chain")

        edge_in = [sem(f"edge_in{k}") for k in range(EDGE_SLOTS)]
        idx_copied = sem("idx_copied")
        x_in = [sem(f"x_in{k}") for k in range(GATHER_SLOTS)]
        onehot_ready = sem("onehot_ready")
        chunk_done = sem("chunk_done")
        chunk_added = sem("chunk_added")

        row_idx_set = sem("row_idx_set")
        passed = sem("passed")
        row_in = sem("row_in")
        row_counted = sem("row_counted")
        start_step = sem("start_step")
        start_ready = [sem(f"start_ready{k}") for k in range(2)]
        win_in = [sem(f"win_in{k}") for k in range(2)]
        key_step = sem("key_step")
        keys_ready = sem("keys_ready")
        keys_used = sem("keys_used")
        degree_step = sem("degree_step")
        keys_turned = sem("keys_turned")
        keys_spread = sem("keys_spread")
        hots_ready = sem("hots_ready")
        bank_filled = sem("bank_filled")
        bank_moved = sem("bank_moved")
        x_mm = sem("x_mm")
        x_added = sem("x_added")

        caps_ready = sem("caps_ready")
        caps_summed = sem("caps_summed")
        flag_ready = sem("flag_ready")
        fb_edge_in = sem("fb_edge_in")
        fb_col_in = sem("fb_col_in")
        fb_row_in = sem("fb_row_in")
        fb_x_in = sem("fb_x_in")
        fb_chain = sem("fb_chain")
        fb_chain2 = sem("fb_chain2")
        only_step = sem("only_step")
        fb_moved = sem("fb_moved")
        has_edge_ready = sem("has_edge_ready")
        fb_has_edge_ready = sem("fb_has_edge_ready")
        fb_resid_in = sem("fb_resid_in")
        fb_bias_step = sem("fb_bias_step")
        fb_resid_biased = sem("fb_resid_biased")
        bias_step = sem("bias_step")
        shift_ready = sem("shift_ready")
        dve_y_ready = sem("dve_y_ready")
        var_step = sem("var_step")
        rstd_ready = sem("rstd_ready")
        fb_onehot = sem("fb_onehot")
        fb_mm = sem("fb_mm")
        fb_added = sem("fb_added")
        fb_counted = sem("fb_counted")
        fb_chunk_done = sem("fb_chunk_done")
        resid_free = sem("resid_free")
        resid_in = sem("resid_in")
        resid_biased = sem("resid_biased")
        sums_ready = sem("sums_ready")
        applied_mm = sem("applied_mm")
        applied_moved = sem("applied_moved")
        applied_turned = sem("applied_turned")
        resid_ready = sem("resid_ready")
        stats_done = sem("stats_done")
        var_ready = sem("var_ready")
        std_ready = sem("std_ready")
        y_ready = sem("y_ready")
        out_done = sem("out_done")

        edge_rows = edge_attr[0:OWN, :].rearrange("(c p j) d -> c p j d", p=P, j=J)
        edge_last = edge_attr[E - CH:E, :].rearrange("(p j) d -> p j d", j=J)
        dst_chunks = dst[0:OWN].rearrange("(c e) -> c e", e=CH)
        src_chunks = src[0:OWN].rearrange("(c e) -> c e", e=CH)
        x_pairs = x.rearrange("(g p h) d -> p g h d", p=PB, h=WN)
        out_pairs = out.rearrange("(g p h) d -> g p h d", p=PB, h=WN)

        def at_least(eng, s, n):
            if not isinstance(n, int) or n > 0:
                eng.wait_ge(s, n)

        def in_turn(eng, count, step):
            step(0, 0, 0, False)
            step(1, 0, 1, False)
            with eng.Fori(0, (count - 3) // 2) as i:
                step(i * 2 + 2, i + 1, 0, False)
                step(i * 2 + 3, i + 1, 1, False)
            step(count - 1, (count - 1) // 2, 0, True)

        def chunks_of(last):
            segs, pos = [], 0
            for seg in SEG_CHUNKS:
                mine = []
                for kind, n in seg:
                    if kind == "A" or not last or n < LAST_B:
                        mine.append((kind, n, pos))
                        pos += 1
                segs.append(mine)
            return segs

        def chunk_id(m, kind, n):
            return m * A_ROUND + n if kind == "A" else m * B_ROUND + n + CA

        def after(m, last, pos, ahead):
            flat = [c for seg in chunks_of(last) for c in seg]
            if pos + ahead < len(flat):
                kind, n, _ = flat[pos + ahead]
                return m, kind, n
            if last:
                return None
            kind, n, _ = [c for seg in chunks_of(False) for c in seg][pos + ahead - len(flat)]
            return m + 1, kind, n

        A_POS = [pos for seg in chunks_of(False) for kind, n, pos in seg if kind == "A"]
        BLOCK_CUTS = [XB * s // SEGS for s in range(SEGS + 1)]

        def rows_before(half, odd):
            return half * 3 + (4 if odd else 2)

        block = ctx.enter_context(nc.Block())

        @block.sync
        def _(sp):
            sp.dma_start(src_col[:, 0:A_ROUND, :], src[0:A_ROUND * CH].rearrange("(c p j) -> p c j", p=P, j=J)).then_inc(src_first_in, 16)
            with nc.allow_non_contiguous_dma(reason="single destinations at a stride"):
                sp.dma_start(firsts_int.rearrange("a (r e) -> a r e", e=1), dst.rearrange("(a r e) -> a r e", a=1, e=ROW)[:, :, 0:1]).then_inc(firsts_in, 16)
                sp.dma_start(chunk_firsts[:, 0:NFULL].rearrange("a (r e) -> a r e", e=1), dst[0:OWN].rearrange("(a r e) -> a r e", a=1, e=CH)[:, :, 0:1]).then_inc(firsts_in, 16)
            sp.dma_start(chunk_firsts[:, NFULL:NCH], dst[OWN:OWN + 1].rearrange("(a b) -> a b", a=1)).then_inc(firsts_in, 16)
            sp.dma_start(dst_nat[:, 0, :], dst[0:P * CH].rearrange("(c e) -> c e", e=CH)).then_inc(dst_in, 16)
            sp.dma_start(dst_nat[0:T1 - 1, 1, :], dst[P * CH:OWN].rearrange("(c e) -> c e", e=CH)).then_inc(dst_in, 16)
            sp.dma_start(dst_nat[T1 - 1:T1, 1, :], dst[E - CH:E].rearrange("(c e) -> c e", e=CH)).then_inc(dst_in, 16)
            with nc.allow_non_contiguous_dma(reason="single destinations at a stride"):
                sp.dma_start(first_col_int[:, 0:1], dst[0:P * CH].rearrange("(c e) -> c e", e=CH)[:, 0:1]).then_inc(dst_in, 16)
            with nc.allow_non_contiguous_dma(reason="single destinations at a stride"):
                sp.dma_start(first_col_int[0:T1 - 1, 1:2], dst[P * CH:OWN].rearrange("(c e) -> c e", e=CH)[:, 0:1]).then_inc(dst_in, 16)
            sp.dma_start(first_col_int[T1 - 1:T1, 1:2], dst[OWN:OWN + 1].rearrange("(a b) -> a b", a=1)).then_inc(dst_in, 16)

            for w, a in enumerate((w_node, w_edge, w_msg)):
                sp.dma_start(weights[:, w, :], a).then_inc(small_in, 16)
            for w, a in enumerate((b_node, b_edge)):
                sp.dma_start(bias_col[:, w:w + 1], a.rearrange("(d a) -> d a", a=1)).then_inc(small_in, 16)
            sp.dma_start(bias_m[:, :], b_msg.rearrange("(a d) -> a d", a=1)).then_inc(small_in, 16)

            def load(m, half, odd, last):
                for seg in chunks_of(last):
                    for kind, n, pos in seg:
                        t = m * PER_ROUND + pos
                        k = pos % EDGE_SLOTS
                        at_least(sp, chunk_done, t - EDGE_SLOTS + 1)
                        final = last and kind == "B" and n == LAST_B - 1
                        sp.dma_start(edges[:, k, :, :], edge_last if final else edge_rows[chunk_id(m, kind, n)]).then_inc(edge_in[k], 16)
                        if isinstance(m, int) and m == 0 and pos == 1:
                            sp.dma_start(src_col[:, A_ROUND:CA, :], src[A_ROUND * CH:CA * CH].rearrange("(c p j) -> p c j", p=P, j=J)).then_inc(src_in, 16)
                            sp.wait_ge(x_zeroed, 1)
                            whole = N // P
                            sp.dma_start(x_raw[:, 0:whole * D].rearrange("p (b d) -> p b d", d=D), x[0:whole * P, :].rearrange("(b p) d -> p b d", p=P)).then_inc(x_raw_in, 16)
                            sp.dma_start(x_raw[0:N - whole * P, whole * D:XB * D], x[whole * P:N, :]).then_inc(x_raw_in, 16)

            in_turn(sp, ROUNDS, load)
            sp.wait_ge(x_mm, ROUNDS - 1)
            sp.dma_start(resid.rearrange("p (g h) d -> p g h d", h=WN), x_pairs).then_inc(resid_in, 16)

            sp.wait_ge(flag_ready, 1)
            flag = sp.value_load(flag_int[0:1, 0:1], min_val=0, max_val=1)
            with sp.If(flag > 0):
                sp.wait_ge(resid_biased, SPANS + 1)
                sp.dma_start(resid.rearrange("p (g h) d -> p g h d", h=WN), x_pairs).then_inc(fb_resid_in, 16)

                def fb_load(c, edge_part, dst_part, src_part):
                    sp.wait_ge(fb_chunk_done, c + 1)
                    sp.dma_start(edges[:, 0, :, :], edge_part).then_inc(fb_edge_in, 16)
                    sp.dma_start(fb_dst_int, dst_part.rearrange("a (p j) -> p (a j)", j=J)).then_inc(fb_col_in, 16)
                    sp.dma_start(fb_src_int, src_part.rearrange("a (p j) -> p (a j)", j=J)).then_inc(fb_col_in, 16)
                    sp.dma_start(fb_row_int, dst_part.to_broadcast([PB, CH])).then_inc(fb_row_in, 16)
                with sp.Fori(0, NFULL) as c:
                    fb_load(c, edge_rows[c], dst_chunks[bass.ds(c, 1), :], src_chunks[bass.ds(c, 1), :])
                fb_load(NFULL, edge_last, dst[E - CH:E].rearrange("(a e) -> a e", a=1), src[E - CH:E].rearrange("(a e) -> a e", a=1))

            with sp.Fori(0, SPANS - 1) as s:
                sp.wait_ge(y_ready, (s + 1) * (SPAN * WN))
                sp.dma_start(out_pairs[bass.ds(s * SPAN, SPAN)].rearrange("g p h d -> p g h d"),
                             resid[:, bass.ds(s * (SPAN * WN), SPAN * WN), :].rearrange("p (g h) d -> p g h d", h=WN)).then_inc(out_done, 16)
            sp.wait_ge(y_ready, (SPANS - 1) * SPAN * WN + ACT_SHARE)
            sp.wait_ge(dve_y_ready, SPAN * WN - ACT_SHARE)
            sp.dma_start(out_pairs[(SPANS - 1) * SPAN:GROUPS].rearrange("g p h d -> p g h d"),
                         resid[:, (SPANS - 1) * SPAN * WN:GROUPS * WN, :].rearrange("p (g h) d -> p g h d", h=WN)).then_inc(out_done, 16)
            sp.wait_ge(out_done, SPANS * 16)

        @block.gpsimd
        def _(pool):
            pool.iota(iota_bf[:, :], pattern=[[1, P]], base=0, channel_multiplier=0, allow_small_or_imprecise_dtypes=True).then_inc(consts, 1)
            pool.iota(iota_we[:, :], pattern=[[1, P]], base=0, channel_multiplier=0, allow_small_or_imprecise_dtypes=True).then_inc(consts, 1)
            pool.iota(iota_p[:, :], pattern=[[0, 1]], base=0, channel_multiplier=1, allow_small_or_imprecise_dtypes=True).then_inc(consts, 1)
            pool.iota(penalty, pattern=[[1, CH]], base=0, channel_multiplier=0, allow_small_or_imprecise_dtypes=True).then_inc(consts, 1)
            pool.iota(window_node[:, :], pattern=[[NB, GROUPS + 1]], base=0, channel_multiplier=WN, allow_small_or_imprecise_dtypes=True).then_inc(consts, 1)

            def pass_waits():
                pool.sem_inc(passed, 1)

            def gather(slot, columns, copied, copied_value, done):
                pool.tensor_copy(src_idx[:, slot, :], columns).then_inc(copied, 1)
                pool.wait_ge(copied, copied_value)
                pass_waits()
                for j in range(J):
                    pool.indirect_dma_start(out=gathered[:, slot, j, :], out_offset=None, in_=x[:, :],
                                            in_offset=bass.IndirectOffsetOnAxis(ap=src_idx[:, slot, j:j + 1], axis=0)).then_inc(done, 16)

            def gather_chunk(m, n):
                slot = n % GATHER_SLOTS
                if n >= GATHER_SLOTS:
                    at_least(pool, chunk_done, m * PER_ROUND + A_POS[n - GATHER_SLOTS] + 1)
                else:
                    at_least(pool, chunk_done, (m - 1) * PER_ROUND + A_POS[A_ROUND + n - GATHER_SLOTS] + 1)
                pass_waits()
                gather(slot, src_col[:, bass.ds(m * A_ROUND + n, 1), :].rearrange("p a j -> p (a j)"), idx_copied,
                       m * A_ROUND + n + 1, x_in[slot])

            def search_row(job, group):
                at_least(pool, row_counted, job)
                pass_waits()
                pool.tensor_copy(row_idx[:, :], row_start_int[:, bass.ds(group, 1)]).then_inc(row_idx_set, 1)
                pool.wait_ge(row_idx_set, job + 1)
                pass_waits()
                pool.indirect_dma_start(out=rows[:, :], out_offset=None, in_=dst.rearrange("(r e) -> r e", e=ROW),
                                        in_offset=bass.IndirectOffsetOnAxis(ap=row_idx[:, 0:1], axis=1)).then_inc(row_in, 16)

            def load_windows(kind, number, arrays):
                pool.wait_ge(start_ready[kind], number + 1)
                pass_waits()
                for to, array in arrays:
                    pool.indirect_dma_start(out=to[:, :], out_offset=None, in_=array.rearrange("(r e) -> r e", e=WE),
                                            in_offset=bass.IndirectOffsetOnAxis(ap=start_int[kind][:, 0:1], axis=1)).then_inc(win_in[kind], 16)

            def step(m, half, odd, last):
                job = rows_before(half, odd)
                for s in range(SEGS):
                    if s < A_ROUND and not (isinstance(m, int) and m == 0 and s < GATHER_SLOTS):
                        if isinstance(m, int) and m == 0 and s == GATHER_SLOTS:
                            pool.wait_ge(src_in, 16)
                        gather_chunk(m, s)
                    if s == 0 and not last:
                        load_windows(0, m + 1, ((win_dst[0], dst), (win_src, src)))
                    if s == 1 and not odd and not last:
                        search_row(job, half)
                    if s == 2 and not last:
                        search_row(job + (0 if odd else 1), m + (G0 + 2))
                    if s == 4 and not odd and not last:
                        load_windows(1, half, ((win_dst[1], dst),))

            pool.wait_ge(src_first_in, 16)
            gather_chunk(0, 0)
            pool.wait_ge(offsets_ready, 1)
            search_row(0, G0)
            pool.memset(sums[:, 0, :], 0.0).then_inc(sums_zeroed, 1)
            search_row(1, G0 + 1)
            load_windows(0, 0, ((win_dst[0], dst), (win_src, src)))
            gather_chunk(0, 1)
            pool.wait_ge(offsets_ready, 3)
            in_turn(pool, ROUNDS, step)

            def add_bias(made, done):
                with pool.Fori(0, SPANS) as s:
                    shape = [PB, SPAN * WN, D]
                    pool.wait_ge(done, s + 1)
                    pool.tensor_tensor(bias_rows, has_edge[:, bass.ds(s * (SPAN * WN), SPAN * WN)].rearrange("p (k a) -> p k a", a=1).to_broadcast(shape),
                                       bias_row[:, :].rearrange("p (a d) -> p a d", a=1).to_broadcast(shape), ALU.mult).then_inc(made, 1)
                    pool.wait_ge(made, s + 1)
                    span = resid[:, bass.ds(s * (SPAN * WN), SPAN * WN), :]
                    pool.tensor_tensor(span, span, bias_rows, ALU.add).then_inc(done, 1)

            pool.wait_ge(has_edge_ready, 1)
            pool.wait_ge(chunk_done, NCH)
            pool.sem_inc(resid_biased, 1)
            pool.wait_ge(resid_in, 16)
            add_bias(bias_step, resid_biased)

            pool.wait_ge(flag_ready, 1)
            flag = pool.value_load(flag_int[0:1, 0:1], min_val=0, max_val=1)
            with pool.If(flag > 0):
                with pool.Fori(0, NCH) as c:
                    pool.wait_ge(fb_chunk_done, c + 1)
                    pool.wait_ge(fb_col_in, (c + 1) * 32)
                    pass_waits()
                    gather(0, fb_src_int, idx_copied, c + (CA + 1), fb_x_in)
                pool.wait_ge(fb_has_edge_ready, 1)
                pool.sem_inc(fb_resid_biased, 1)
                pool.wait_ge(fb_resid_in, 16)
                add_bias(fb_bias_step, fb_resid_biased)

        @block.tensor
        def _(pe):
            pe.wait_ge(firsts_ready, 1)
            pe.matmul(count_ps[2][:, 0:NROW], ones[0:1, :], scratch[0:1, :], start=True, stop=True).then_inc(firsts_spread, 1)
            pe.wait_ge(small_in, 96)
            pe.wait_ge(ident_ready, 2)
            pe.transpose(turn_ps[:, 0:D], weights[:, 2, :], ident[:, :]).then_inc(wm_turned, 1)
            pe.wait_ge(rel_nat_ready, 1)
            for t, n in ((0, P), (1, T1)):
                turned = count_ps[t][:, :].bitcast(BF16).rearrange("p (j c) -> p j c", j=J)
                for j in range(J):
                    mm = pe.transpose(turned[:, j, 0:n], rel_nat[0:n, t, j:CH:J], ident_bf[0:n, 0:n])
            mm.then_inc(rel_turned, 1)

            pe.wait_ge(wm_ready, 1)
            for k in range(2):
                pe.matmul(turn_ps[:, k * D:(k + 1) * D], weights[:, k, :], wm_t[:, :], start=True, stop=True)
            pe.matmul(turn_ps[0:PB, 2 * D:3 * D], bias_rep[:, 0:PB], wm_t[:, :], start=True, stop=False)
            pe.matmul(turn_ps[0:PB, 2 * D:3 * D], ones[0:1, 0:PB], bias_m[:, :], start=False, stop=True).then_inc(weights_mm, 1)

            def chunk_matmuls(bank, kinds, hot):
                for kind, rows_of in kinds:
                    for j in range(J):
                        mm = pe.matmul(bank[:, kind * W:(kind + 1) * W], rows_of[:, j, :], hot[:, j, :], start=(j == 0), stop=(j == J - 1))
                return mm

            def chunk(m, kind, n, pos):
                t = m * PER_ROUND + pos
                k = pos % EDGE_SLOTS
                pe.wait_ge(onehot_ready, t + 1)
                at_least(pe, chunk_added, t - CHUNK_BANKS + 1)
                pe.wait_ge(edge_in[k], (m * (PER_ROUND // EDGE_SLOTS) + (pos // EDGE_SLOTS + 1)) * 16)
                kinds = [(1, edges[:, k, :, :])]
                if kind == "A":
                    slot = n % GATHER_SLOTS
                    pe.wait_ge(x_in[slot], (m * (A_ROUND // GATHER_SLOTS) + (n // GATHER_SLOTS + 1)) * (16 * J))
                    kinds.append((0, gathered[:, slot, :, :]))
                chunk_matmuls(chunk_ps[pos % CHUNK_BANKS], kinds, onehot[:, pos % ONEHOT_SLOTS, :, :]).then_inc(chunk_done, 1)

            pe.wait_ge(prologue_done, 1)

            def turn_keys(m):
                pe.wait_ge(keys_ready, m + 1)
                at_least(pe, keys_spread, m)
                turned = turn_ps[:, :].bitcast(BF16)
                pe.transpose(turned[0:WE, 0:PB], row_bf[:, :], ident_bf[0:PB, 0:PB])
                pe.transpose(turned[0:WE, P:P + PB], key_bf[:, :], ident_bf[0:PB, 0:PB]).then_inc(keys_turned, 1)

            def count_batch(m, odd, s):
                pe.wait_ge(hots_ready, m * SEGS + (s + 1))
                slot = (SEGS * odd + s) % 2
                for f in range(FILLS):
                    fill = s * FILLS + f
                    bank = fill % M_BANKS
                    if fill >= M_BANKS:
                        pe.wait_ge(bank_moved, m * (SEGS * FILLS) + (fill - M_BANKS + 1))
                    else:
                        before = max(q for q in range(SEGS * FILLS) if q % M_BANKS == bank)
                        at_least(pe, bank_moved, (m - 1) * (SEGS * FILLS) + (before + 1))
                    for w in range(FILL):
                        win = f * FILL + w
                        mm = pe.matmul(count_ps[bank][:, w * KEYS:(w + 1) * KEYS], row_hot[0:WE, slot, win, :], key_hot[0:WE, slot, win, 0:KEYS],
                                       start=True, stop=True)
                    mm.then_inc(bank_filled, 1)

            def apply_x(g, odd, s):
                if s == 0:
                    pe.wait_ge(bank_moved, (g + 1) * (SEGS * FILLS))
                    at_least(pe, x_added, g)
                for b in range(BLOCK_CUTS[s], BLOCK_CUTS[s + 1]):
                    for part in range(3):
                        mm = pe.matmul(x_ps[:, 0:NB], x_parts[:, part, b, :], counts[odd][:, b, :],
                                       start=(b == 0 and part == 0), stop=(b == XB - 1 and part == 2))
                if s == SEGS - 1:
                    mm.then_inc(x_mm, 1)

            def step(m, half, odd, last):
                first = isinstance(m, int) and m == 0
                for s, seg in enumerate(chunks_of(last)):
                    for kind, n, pos in seg:
                        chunk(m, kind, n, pos)
                        if first and pos == CHUNK_BANKS - 1:
                            turn_keys(0)
                    count_batch(m, odd, s)
                    if isinstance(m, int) and m == 1 and s == 0:
                        pe.wait_ge(x_lo, XB // SPLIT_BLOCKS)
                    if not first:
                        apply_x(m - 1, 1 - odd, s)
                    if s == 2 and not last:
                        turn_keys(m + 1)

            in_turn(pe, ROUNDS, step)
            pe.wait_ge(caps_ready, 1)
            sums_of = chunk_ps[0]
            pe.wait_ge(chunk_added, NCH)
            pe.matmul(sums_of[0:1, 0:2], ones[:, 0:1], captured[:, 0:2], start=True, stop=True)
            pe.matmul(sums_of[0:1, 2:3], ones[0:CA, 0:1], captured[0:CA, 0:1], start=True, stop=True)
            pe.matmul(sums_of[0:1, 3:3 + ROUNDS], ones[0:PB, 0:1], captured[0:PB, 2:2 + ROUNDS], start=True, stop=True)
            pe.matmul(sums_of[0:1, 64:64 + WN * GROUPS], ones[0:PB, 0:1], degree[:, :], start=True, stop=True).then_inc(caps_summed, 1)
            for s in range(SEGS):
                apply_x(ROUNDS - 1, 0, s)

            pe.wait_ge(flag_ready, 1)
            flag = pe.value_load(flag_int[0:1, 0:1], min_val=0, max_val=1)
            with pe.If(flag > 0):
                with pe.Fori(0, NCH) as c:
                    with pe.Fori(0, WINDOWS) as w:
                        pe.wait_ge(fb_edge_in, (c + 1) * 16)
                        pe.wait_ge(fb_x_in, (c + 1) * (16 * J))
                        pe.wait_ge(fb_onehot, c * WINDOWS + w + 1)
                        chunk_matmuls(chunk_ps[0], [(1, edges[:, 0, :, :]), (0, gathered[:, 0, :, :])], onehot[:, 0, :, :]).then_inc(fb_mm, 1)

            def apply_weights(g, i):
                if i != 1:
                    pe.wait_ge(applied_moved, g + 1 if i == 0 else g)
                for k in range(2):
                    mm = pe.matmul(count_ps[i % 2][:, 0:NB], w_both[:, k, :], sums[:, k, bass.ds(g * NB, NB)], start=(k == 0), stop=(k == 1))
                mm.then_inc(applied_mm, 1)

            def turn_applied(g, i):
                pe.wait_ge(applied_moved, g + 2)
                if i != 1:
                    pe.wait_ge(resid_ready, (g + 1 if i == 0 else g) * WN)
                for h in range(WN):
                    mm = pe.transpose(count_ps[2 + i % 2][0:PB, h * D:(h + 1) * D], applied[i % 2][:, h:NB:WN], ident[:, :])
                mm.then_inc(applied_turned, 1)

            pe.wait_ge(sums_ready, 1)
            with pe.Fori(0, SPANS) as s:
                for i in range(SPAN):
                    apply_weights(s * SPAN + i, i)
                    if i > 0:
                        turn_applied(s * SPAN + (i - 1), i - 1)
                turn_applied(s * SPAN + (SPAN - 1), SPAN - 1)

        @block.vector
        def _(dve):
            steps = [0]

            def link(ins):
                steps[0] += 1
                ins.then_inc(dve_chain, 1)
                dve.wait_ge(dve_chain, steps[0])

            dve.memset(ones[:, :], 1.0)
            dve.memset(captured[:, :], 0.0)
            link(dve.memset(x_raw[:, (XB - 1) * D:XB * D], 0.0))
            dve.sem_inc(x_zeroed, 1)
            dve.wait_ge(consts, 5)
            dve.tensor_scalar(node_half[:, :], window_node[:, :], -0.5, None, ALU.add).then_inc(half_ready, 1)
            dve.tensor_scalar(ident[:, :], iota_we[:, :], iota_p[:, 0:1], None, ALU.is_equal).then_inc(ident_ready, 1)
            dve.tensor_scalar(ident_bf[:, :], iota_we[:, :], iota_p[:, 0:1], None, ALU.is_equal).then_inc(ident_ready, 1)
            dve.wait_ge(firsts_in, 48)
            dve.tensor_copy(scratch[0:1, :], firsts_int[:, :]).then_inc(firsts_ready, 1)
            link(dve.tensor_scalar(base_int[:, :], chunk_firsts, float(NP - W), 0.0, ALU.min, ALU.max))

            dve.wait_ge(dst_in, 96)
            dve.tensor_scalar(is_last[:, :], iota_p[:, :], float(T1 - 1), 1.0e5, ALU.is_equal, ALU.mult)
            link(dve.tensor_scalar(first_col[:, 0:1], first_col_int[:, 0:1], float(NP - W), None, ALU.min))
            link(dve.tensor_scalar(first_col[0:T1, 1:2], first_col_int[0:T1, 1:2], float(NP - W), None, ALU.min))
            link(dve.tensor_scalar(penalty[0:T1, :], penalty[0:T1, :], float(REPEATED), is_last[0:T1, 0:1], ALU.is_lt, ALU.mult))
            dve.tensor_scalar(rel_nat[:, 0, :], dst_nat[:, 0, :], first_col[:, 0:1], None, ALU.subtract)
            link(dve.scalar_tensor_tensor(rel_nat[0:T1, 1, :], dst_nat[0:T1, 1, :], first_col[0:T1, 1:2], penalty[0:T1, :], ALU.subtract, ALU.subtract))
            dve.sem_inc(rel_nat_ready, 1)

            def row_starts(g0, g1):
                at = row_start[:, g0:g1]
                link(dve.tensor_scalar(at, row_count[:, g0:g1], float(ROW) / 2, float(NROW) * ROW / 2 - ROW, ALU.mult, ALU.add))
                link(dve.tensor_scalar(at, at, 0.0, float(E - ROW), ALU.max, ALU.min))
                link(dve.tensor_copy(row_start_int[:, g0:g1], at))
                link(dve.tensor_scalar(row_middle[:, g0:g1], at, float(ROW // 2), None, ALU.add))
                dve.sem_inc(offsets_ready, 1)

            dve.wait_ge(rows_before_ready, 2)
            row_starts(G0, G0 + 2)

            dve.wait_ge(small_in, 96)
            dve.wait_ge(wm_turned, 1)
            dve.tensor_copy(wm_t[:, :], turn_ps[:, 0:D])
            link(dve.tensor_scalar(bias_rep[:, :], ones[:, :], bias_col[:, 0:1], bias_col[:, 1:2], ALU.mult, ALU.add))
            dve.sem_inc(wm_ready, 1)
            dve.wait_ge(rel_turned, 1)
            for t, n in ((0, P), (1, T1)):
                turned = count_ps[t][:, :].bitcast(BF16).rearrange("p (j c) -> p c j", j=J)
                link(dve.tensor_copy(rel_col[:, t * P:t * P + n, :], turned[:, 0:n, :]))
            dve.wait_ge(weights_mm, 1)
            dve.tensor_copy(w_both[:, :, :], turn_ps[:, 0:2 * D].rearrange("p (k d) -> p k d", k=2))
            link(dve.tensor_copy(bias_row[:, :], turn_ps[0:PB, 2 * D:3 * D]))
            dve.sem_inc(prologue_done, 1)

            def count_captured():
                inside = penalty.bitcast(BF16)[:, 0:CH]
                for t, n in ((0, P), (1, T1)):
                    link(dve.tensor_scalar(inside[0:n, :], rel_nat[0:n, t, :], 0.0, None, ALU.is_ge))
                    link(dve.scalar_tensor_tensor(inside[0:n, :], rel_nat[0:n, t, :], float(W), inside[0:n, :], ALU.is_lt, ALU.mult,
                                                  accum_out=captured[0:n, t:t + 1]))

            def find_start(job, kind, group):
                dve.wait_ge(row_counted, job + 1)
                dve.scalar_tensor_tensor(start_tmp[:, :], sign_sum[:, :], 0.5, row_middle[:, bass.ds(group, 1)], ALU.mult, ALU.add).then_inc(start_step, 1)
                dve.wait_ge(start_step, job * 2 + 1)
                dve.tensor_scalar(start[kind][:, :], start_tmp[:, :], float(E - WE), 0.0, ALU.min, ALU.max).then_inc(start_step, 1)
                dve.wait_ge(start_step, job * 2 + 2)
                dve.tensor_copy(start_int[kind][:, :], start[kind][:, :]).then_inc(start_ready[kind], 1)

            def count_degree(kind, group, unit):
                for h in range(WN):
                    dve.tensor_scalar(held[:, h, :], rel_key[:, :], float(unit * h), None, ALU.is_equal, ALU.add,
                                      accum_out=degree[:, bass.ds(group * WN + h, 1)]).then_inc(degree_step, 1)

            def make_keys(m, jobs):
                group = m + G0
                dve.wait_ge(win_in[0], (m + 1) * 32)
                at_least(dve, keys_turned, m)
                dve.tensor_scalar(src_block[:, :], win_src[:, :], 7, None, ALU.logical_shift_right).then_inc(key_step, 1)
                dve.tensor_scalar(src_row[:, :], win_src[:, :], P - 1, None, ALU.bitwise_and).then_inc(key_step, 1)
                at_least(dve, degree_step, jobs * WN)
                dve.tensor_scalar(rel_key[:, :], win_dst[0][:, :], window_node[:, bass.ds(group, 1)], float(XB), ALU.subtract, ALU.mult).then_inc(key_step, 1)
                dve.tensor_scalar(early_edge[:, :], iota_we[0:PB, 0:WE], start[0][:, 0:1], float(CA * CH), ALU.add, ALU.is_lt).then_inc(key_step, 1)
                dve.wait_ge(key_step, m * 6 + 4)
                dve.tensor_tensor(key[:, :], rel_key[:, :], src_block[:, :], ALU.add).then_inc(key_step, 1)
                dve.tensor_copy(row_bf[:, :], src_row[:, :]).then_inc(key_step, 1)
                dve.wait_ge(key_step, m * 6 + 6)
                dve.scalar_tensor_tensor(key_bf[:, :], early_edge[:, :], 1024.0, key[:, :], ALU.mult, ALU.add).then_inc(keys_ready, 1)
                count_degree(0, group, XB)
                dve.wait_ge(degree_step, jobs * WN + WN)
                dve.wait_ge(keys_ready, m + 1)
                dve.tensor_scalar(held[:, WN, :], key_bf[:, :], 0.0, None, ALU.is_ge).then_inc(keys_used, 1)
                dve.wait_ge(keys_used, m * 2 + 1)
                dve.scalar_tensor_tensor(held[:, WN, :], key_bf[:, :], float(KEYS), held[:, WN, :], ALU.is_lt, ALU.mult,
                                         accum_out=captured[0:PB, bass.ds(m + 2, 1)]).then_inc(keys_used, 1)
                dve.wait_ge(keys_used, m * 2 + 2)

            def only_degrees(k, jobs):
                dve.wait_ge(win_in[1], (k + 1) * 16)
                at_least(dve, degree_step, jobs * WN)
                dve.tensor_scalar(rel_key[:, :], win_dst[1][:, :], window_node[:, bass.ds(k, 1)], None, ALU.subtract).then_inc(only_step, 1)
                dve.wait_ge(only_step, k + 1)
                count_degree(1, k, 1)

            def degrees_before(half, odd):
                return half * 3 + (3 if odd else 1)

            def make_hots(m, odd, s):
                slot = (SEGS * odd + s) % 2
                if s == 0:
                    dve.wait_ge(keys_spread, m + 1)
                at_least(dve, bank_filled, m * (SEGS * FILLS) + (s - 1) * FILLS)
                for hot, four, width in ((row_hot, row4, P), (key_hot, key4, KPAD)):
                    shape = [WE, BATCH, width // 4, 4]
                    ins = dve.tensor_tensor(hot[0:WE, slot, :, :].rearrange("p w (a b) -> p w a b", b=4),
                                            iota_bf[0:WE, 0:width].rearrange("p (c a b) -> p c a b", c=1, b=4).to_broadcast(shape),
                                            four[0:WE, odd, s * BATCH:(s + 1) * BATCH, :].rearrange("p w (a b) -> p w a b", a=1).to_broadcast(shape),
                                            ALU.is_equal)
                ins.then_inc(hots_ready, 1)

            def make_onehot(m, kind, n, pos):
                t = m * PER_ROUND + pos
                at_least(dve, chunk_done, t - ONEHOT_SLOTS + 1)
                rel = rel_col[:, bass.ds(chunk_id(m, kind, n), 1), :]
                dve.tensor_tensor(onehot[:, pos % ONEHOT_SLOTS, :, :], iota_bf[:, 0:W].rearrange("p (a w) -> p a w", a=1).to_broadcast([P, J, W]),
                                  rel.rearrange("p a j -> p j a").to_broadcast([P, J, W]), ALU.is_equal).then_inc(onehot_ready, 1)

            def add_chunk(m, kind, n, pos, groups_added):
                t = m * PER_ROUND + pos
                at = dve.value_load(base_int[0:1, bass.ds(chunk_id(m, kind, n), 1)], min_val=0, max_val=NP - W)
                at_least(dve, chunk_added, t)
                at_least(dve, x_added, groups_added)
                dve.wait_ge(chunk_done, t + 1)
                k0, kn = (0, 2) if kind == "A" else (1, 1)
                to = sums[:, k0:2, bass.ds(at, W)]
                dve.tensor_tensor(to, to, chunk_ps[pos % CHUNK_BANKS][:, k0 * W:2 * W].rearrange("p (k w) -> p k w", k=kn), ALU.add).then_inc(chunk_added, 1)

            def add_group(g, chunks):
                at_least(dve, chunk_added, chunks)
                dve.wait_ge(x_mm, g + 1)
                to = sums[:, 0, bass.ds((g + G0) * NB, NB)]
                dve.tensor_tensor(to, to, x_ps[:, 0:NB], ALU.add).then_inc(x_added, 1)

            def split_rest(to, part, seen, signal):
                wide = SPLIT_BLOCKS * D
                for k in range(XB // SPLIT_BLOCKS):
                    dve.wait_ge(seen, k + 1)
                    dve.tensor_tensor(to(k), x_raw[:, k * wide:(k + 1) * wide],
                                      x_parts[:, part, k * SPLIT_BLOCKS:(k + 1) * SPLIT_BLOCKS, :].rearrange("p b d -> p (b d)"),
                                      ALU.subtract).then_inc(signal, 1)

            def step(m, half, odd, last):
                first = isinstance(m, int) and m == 0
                second = isinstance(m, int) and m == 1
                groups_added = m - 1 if not (first or second) else 0
                for s, seg in enumerate(chunks_of(last)):
                    if s == 0 and not first and not second:
                        add_group(m - 2, m * PER_ROUND - 1)
                    for kind, n, pos in seg:
                        ahead = after(m, last, pos, ONEHOT_SLOTS - 1)
                        if ahead is not None:
                            am, akind, an = ahead
                            flat = pos + ONEHOT_SLOTS - 1
                            over = flat >= PER_ROUND and not last
                            make_onehot(am, akind, an, flat - PER_ROUND if over else flat)
                        if pos > 0:
                            back = [c for sg in chunks_of(last) for c in sg][pos - 1]
                            add_chunk(m, back[0], back[1], back[2], groups_added)
                        elif not first:
                            back = [c for sg in chunks_of(False) for c in sg][-1]
                            add_chunk(m - 1, back[0], back[1], back[2], groups_added)
                    if s < SEGS - 1:
                        make_hots(m, odd, s + 1)
                    elif not last:
                        make_hots(m + 1, 1 - odd, 0)
                    if s == 0 and odd:
                        only_degrees(half, degrees_before(half, 1) - 1)
                    if s == 1 and not last:
                        make_keys(m + 1, degrees_before(half, odd))
                    if s == 2 and not odd and not last:
                        find_start(rows_before(half, 0), 1, half)
                    if s == 3 and not last:
                        find_start(rows_before(half, odd) + (0 if odd else 1), 0, m + (G0 + 2))
                    if first and s == 0:
                        split_rest(lambda k: x_raw[:, k * SPLIT_BLOCKS * D:(k + 1) * SPLIT_BLOCKS * D], 0, x_hi, x_rest)
                    if first and s == 2:
                        split_rest(lambda k: x_parts[:, 2, k * SPLIT_BLOCKS:(k + 1) * SPLIT_BLOCKS, :].rearrange("p b d -> p (b d)"), 1, x_mid, x_lo)

            make_onehot(0, "A", 0, 0)
            make_onehot(0, "B", 0, 1)
            link(dve.memset(sums[:, 1, :], 0.0))
            find_start(0, 0, G0)
            count_captured()
            make_keys(0, 0)
            find_start(1, 0, G0 + 1)
            dve.wait_ge(rows_before_ready, GROUPS + 1)
            row_starts(0, G0)
            row_starts(G0 + 2, GROUPS + 1)
            make_hots(0, 0, 0)
            dve.wait_ge(sums_zeroed, 1)
            in_turn(dve, ROUNDS, step)
            flat = [c for sg in chunks_of(True) for c in sg]
            add_chunk(ROUNDS - 1, *flat[-1], ROUNDS - 2)
            dve.wait_ge(degree_step, GROUPS * WN)
            dve.wait_ge(keys_used, ROUNDS * 2)
            dve.sem_inc(caps_ready, 1)
            dve.wait_ge(caps_summed, 1)
            dve.tensor_reduce(totals[:, 0:1], chunk_ps[0][0:1, 0:2], AX.X, ALU.add)
            dve.tensor_reduce(totals[:, 1:2], chunk_ps[0][0:1, 2:3 + ROUNDS], AX.X, ALU.add)
            link(dve.tensor_reduce(totals[:, 2:3], chunk_ps[0][0:1, 64:64 + WN * GROUPS], AX.X, ALU.add))
            link(dve.tensor_scalar(totals[:, 0:3], totals[:, 0:3], float(E), None, ALU.not_equal))
            link(dve.tensor_reduce(totals[:, 3:4], totals[:, 0:3], AX.X, ALU.max))
            dve.tensor_copy(flag_int[:, :], totals[:, 3:4]).then_inc(flag_ready, 1)
            dve.tensor_scalar(has_edge[:, :], degree[:, :], 1.0, None, ALU.min).then_inc(has_edge_ready, 1)
            add_group(ROUNDS - 2, NCH)
            dve.wait_ge(x_added, ROUNDS - 1)
            add_group(ROUNDS - 1, NCH)
            dve.wait_ge(flag_ready, 1)
            dve.wait_ge(x_added, ROUNDS)
            flag = dve.value_load(flag_int[0:1, 0:1], min_val=0, max_val=1)
            with dve.If(flag > 0):
                dve.wait_ge(resid_biased, SPANS + 1)
                dve.memset(sums[:, :, :], 0.0).then_inc(fb_chain, 1)
                dve.memset(degree[:, :], 0.0).then_inc(fb_chain, 1)
                dve.wait_ge(fb_chain, 2)
                dve.sem_inc(fb_chunk_done, 1)

                def fb_chunk(c, last):
                    dve.wait_ge(fb_col_in, (c + 1) * 32)
                    dve.tensor_copy(fb_rel, fb_dst_int).then_inc(fb_moved, 1)
                    if last:
                        dve.wait_ge(fb_moved, c * (WINDOWS + 1) + 1)
                        dve.tensor_scalar(fb_pos, iota_p[:, 0:1].to_broadcast([P, J]), float(J), None, ALU.mult).then_inc(fb_chain, 1)
                        dve.wait_ge(fb_chain, 3)
                        dve.tensor_tensor(fb_pos, fb_pos, iota_we[:, 0:J], ALU.add).then_inc(fb_chain, 1)
                        dve.wait_ge(fb_chain, 4)
                        dve.tensor_scalar(fb_pos, fb_pos, float(REPEATED), -1.0e5, ALU.is_lt, ALU.mult).then_inc(fb_chain, 1)
                        dve.wait_ge(fb_chain, 5)
                        dve.tensor_tensor(fb_rel, fb_rel, fb_pos, ALU.add).then_inc(fb_chain, 1)
                        dve.wait_ge(fb_chain, 6)
                    with dve.Fori(0, WINDOWS) as w:
                        n = c * WINDOWS + w
                        dve.wait_ge(fb_moved, n + c + 1)
                        dve.tensor_tensor(onehot[:, 0, :, :], iota_bf[:, 0:W].rearrange("p (a w) -> p a w", a=1).to_broadcast([P, J, W]),
                                          fb_rel.rearrange("p (j a) -> p j a", a=1).to_broadcast([P, J, W]), ALU.is_equal).then_inc(fb_onehot, 1)
                        dve.wait_ge(fb_onehot, n + 1)
                        dve.tensor_scalar(fb_rel, fb_rel, -float(W), None, ALU.add).then_inc(fb_moved, 1)
                        dve.wait_ge(fb_mm, n + 1)
                        to = sums[:, :, bass.ds(w * W, W)]
                        dve.tensor_tensor(to, to, chunk_ps[0][:, 0:2 * W].rearrange("p (k w) -> p k w", k=2), ALU.add).then_inc(fb_added, 1)
                        dve.wait_ge(fb_added, n + 1)
                    e0 = REPEATED if last else 0
                    dve.wait_ge(fb_row_in, (c + 1) * 16)
                    dve.tensor_copy(fb_row, fb_row_int).then_inc(fb_counted, 1)
                    with dve.Fori(0, WN * GROUPS) as k:
                        n = c * (2 * WN * GROUPS + 1) + k * 2 + 1
                        dve.wait_ge(fb_counted, n)
                        dve.tensor_scalar(fb_equal[:, e0:CH], fb_row[:, e0:CH], fb_node[:, bass.ds(k, 1)], None, ALU.is_equal, ALU.add,
                                          accum_out=start_tmp[:, :]).then_inc(fb_counted, 1)
                        dve.wait_ge(fb_counted, n + 1)
                        dve.tensor_tensor(degree[:, bass.ds(k, 1)], degree[:, bass.ds(k, 1)], start_tmp[:, :], ALU.add).then_inc(fb_counted, 1)
                    dve.wait_ge(fb_counted, (c + 1) * (2 * WN * GROUPS + 1))
                    dve.sem_inc(fb_chunk_done, 1)

                for h in range(WN):
                    dve.tensor_scalar(fb_node.rearrange("p (g h) -> p g h", h=WN)[:, :, h], window_node[:, 0:GROUPS], float(h), None, ALU.add).then_inc(fb_chain2, 1)
                dve.wait_ge(fb_chain2, WN)
                with dve.Fori(0, NFULL) as c:
                    fb_chunk(c, False)
                fb_chunk(NFULL, True)
                dve.tensor_scalar(has_edge[:, :], degree[:, :], 1.0, None, ALU.min).then_inc(fb_has_edge_ready, 1)
                dve.wait_ge(fb_resid_biased, SPANS + 1)

            dve.sem_inc(applied_moved, 1)
            dve.sem_inc(applied_turned, 1)
            dve.sem_inc(resid_ready, WN)
            dve.sem_inc(sums_ready, 1)
            link(dve.tensor_scalar(recip[:, :], degree[:, :], 1.0, None, ALU.max))
            link(dve.reciprocal(recip[:, :], recip[:, :]))

            def add_message(g, i):
                dve.wait_ge(applied_turned, g + 2)
                for h in range(WN):
                    k = g * WN + h
                    row = resid[:, bass.ds(k, 1), :].rearrange("p a d -> p (a d)")
                    dve.scalar_tensor_tensor(row, count_ps[2 + i % 2][0:PB, h * D:(h + 1) * D], recip[:, bass.ds(k, 1)], row, ALU.mult, ALU.add).then_inc(resid_ready, 1)

            def take_stats(g):
                dve.wait_ge(resid_ready, (g + 2) * WN)
                for h in range(WN):
                    k = g * WN + h
                    dve.bn_stats(stats[:, bass.ds(k, 1), :].rearrange("p a s -> p (a s)"),
                                 resid[:, bass.ds(k, 1), :].rearrange("p a d -> p (a d)")).then_inc(stats_done, 1)

            def columns(of, s):
                return of[:, bass.ds(s * (SPAN * WN), SPAN * WN)]

            def make_variance(s):
                dve.wait_ge(stats_done, (s + 1) * (SPAN * WN))
                mine = stats[:, bass.ds(s * (SPAN * WN), SPAN * WN), :]
                gap, var, mu = columns(half_gap, s), columns(var_eps, s), columns(mean, s)
                dve.tensor_tensor(gap, mine[:, :, 1], mine[:, :, 4], ALU.subtract).then_inc(var_step, 1)
                dve.tensor_tensor(var, mine[:, :, 2], mine[:, :, 5], ALU.add).then_inc(var_step, 1)
                dve.tensor_tensor(mu, mine[:, :, 1], mine[:, :, 4], ALU.add).then_inc(var_step, 1)
                dve.wait_ge(var_step, s * 7 + 3)
                dve.tensor_scalar(gap, gap, 0.5, None, ALU.mult).then_inc(var_step, 1)
                dve.tensor_scalar(var, var, 1.0 / D, EPS, ALU.mult, ALU.add).then_inc(var_step, 1)
                dve.tensor_scalar(mu, mu, 0.5, None, ALU.mult).then_inc(var_step, 1)
                dve.wait_ge(var_step, s * 7 + 6)
                dve.tensor_tensor(gap, gap, gap, ALU.mult).then_inc(var_step, 1)
                dve.wait_ge(var_step, s * 7 + 7)
                dve.tensor_tensor(var, var, gap, ALU.add).then_inc(var_ready, 1)

            def make_scale(s):
                dve.wait_ge(std_ready, s + 1)
                dve.reciprocal(columns(rstd, s), columns(stddev, s)).then_inc(rstd_ready, 1)
                dve.wait_ge(rstd_ready, s + 1)
                dve.scalar_tensor_tensor(columns(shift, s), columns(mean, s), -1.0, columns(rstd, s), ALU.mult, ALU.mult).then_inc(shift_ready, 1)

            def span_stats(s, first):
                dve.wait_ge(resid_biased, s + 2)
                for i in range(SPAN):
                    add_message(s * SPAN + i, i)
                    if i == 2 and not first:
                        make_scale(s - 1)
                    if i > 0:
                        take_stats(s * SPAN + (i - 1))
                take_stats(s * SPAN + (SPAN - 1))
                make_variance(s)

            span_stats(0, True)
            with dve.Fori(0, SPANS - 1) as s:
                span_stats(s + 1, False)
            make_scale(SPANS - 1)
            for i in range(ACT_SHARE, SPAN * WN):
                k = (SPANS - 1) * SPAN * WN + i
                dve.tensor_scalar(resid[:, k, :], resid[:, k, :], mean[:, k:k + 1], rstd[:, k:k + 1], ALU.subtract, ALU.mult).then_inc(dve_y_ready, 1)

        @block.scalar
        def _(act):
            def round_part(part, seen, signal):
                wide = SPLIT_BLOCKS * D
                for k in range(XB // SPLIT_BLOCKS):
                    if seen is not None:
                        act.wait_ge(seen, k + 1)
                    act.copy(x_parts[:, part, k * SPLIT_BLOCKS:(k + 1) * SPLIT_BLOCKS, :].rearrange("p b d -> p (b d)"),
                             x_raw[:, k * wide:(k + 1) * wide]).then_inc(signal, 1)

            def count_row(job, group):
                act.wait_ge(row_in, (job + 1) * 16)
                at_least(act, start_step, job * 2)
                act.activation(row_signs[:, :], rows[:, :], ACT.Sign, bias=node_half[:, bass.ds(group, 1)], scale=-1.0,
                               accum_out=sign_sum[:, :]).then_inc(row_counted, 1)

            def spread_keys(m, odd):
                act.wait_ge(keys_turned, m + 1)
                turned = turn_ps[:, :].bitcast(BF16)
                at_least(act, bank_filled, (m - 1) * (SEGS * FILLS))
                for four, at in ((row4, 0), (key4, P)):
                    ins = act.copy(four[0:WE, odd, :, :], turned[0:WE, at:at + PB].rearrange("p (w a) -> p w a", a=1).to_broadcast([WE, PB, 4]))
                ins.then_inc(keys_spread, 1)

            def move_bank(m, odd, fill):
                act.wait_ge(bank_filled, m * (SEGS * FILLS) + (fill + 1))
                act.copy(counts[odd][:, :, fill * FILL * WN:(fill + 1) * FILL * WN],
                         count_ps[fill % M_BANKS][:, 0:FILL * KEYS].rearrange("p (n b) -> p b n", b=XB)).then_inc(bank_moved, 1)

            def step(m, half, odd, last):
                first = isinstance(m, int) and m == 0
                for s in range(SEGS):
                    if s == 0:
                        at_least(act, x_mm, m - 1)
                    if s == 1 and first:
                        round_part(1, x_rest, x_mid)
                    if s == 0 and isinstance(m, int) and m == 1:
                        act.wait_ge(x_lo, XB // SPLIT_BLOCKS)
                    if s == 2 and not odd and not last:
                        count_row(rows_before(half, 0), half)
                    if s == 3 and not last:
                        spread_keys(m + 1, 1 - odd)
                        count_row(rows_before(half, odd) + (0 if odd else 1), m + (G0 + 2))
                    for f in range(FILLS):
                        move_bank(m, odd, s * FILLS + f)

            def count_samples(groups, before):
                for k, g in enumerate(groups):
                    at_least(act, rows_before_ready, before + k)
                    act.activation(row_signs[:, 0:NROW], firsts[0:PB, :], ACT.Sign, bias=node_half[:, g:g + 1], scale=-1.0,
                                   accum_out=row_count[:, g:g + 1]).then_inc(rows_before_ready, 1)

            act.wait_ge(firsts_spread, 1)
            act.copy(firsts, count_ps[2][:, 0:NROW]).then_inc(firsts_copied, 1)
            act.wait_ge(firsts_copied, 1)
            act.wait_ge(half_ready, 1)
            others = [g for g in range(GROUPS + 1) if g not in (G0, G0 + 1)]
            count_samples((G0, G0 + 1), 0)
            count_samples(others[:len(others) // 2], 2)
            act.wait_ge(rows_before_ready, 2 + len(others) // 2)
            act.wait_ge(offsets_ready, 1)
            count_row(0, G0)
            act.wait_ge(row_counted, 1)
            count_samples(others[len(others) // 2:], 2 + len(others) // 2)
            act.wait_ge(rows_before_ready, GROUPS + 1)
            count_row(1, G0 + 1)
            spread_keys(0, 0)
            act.wait_ge(x_raw_in, 32)
            round_part(0, None, x_hi)
            act.wait_ge(prologue_done, 1)
            in_turn(act, ROUNDS, step)

            def move_applied(s, i):
                g = s * SPAN + i
                act.wait_ge(applied_mm, g + 1)
                if i != 1:
                    act.wait_ge(applied_turned, g + 1 if i == 0 else g)
                act.copy(applied[i % 2], count_ps[i % 2][:, 0:NB]).then_inc(applied_moved, 1)

            def take_roots(s):
                act.wait_ge(var_ready, s + 1)
                cols = bass.ds(s * (SPAN * WN), SPAN * WN)
                act.activation(stddev[:, cols], var_eps[:, cols], ACT.Sqrt).then_inc(std_ready, 1)

            def normalize(s, i0, i1):
                act.wait_ge(shift_ready, s + 1)
                for i in range(i0, i1):
                    k = s * (SPAN * WN) + i
                    row = resid[:, bass.ds(k, 1), :].rearrange("p a d -> p (a d)")
                    act.activation(row, row, ACT.Identity, bias=shift[:, bass.ds(k, 1)], scale=rstd[:, bass.ds(k, 1)]).then_inc(y_ready, 1)

            for s in range(SPANS + 1):
                for i in range(SPAN):
                    if s < SPANS:
                        move_applied(s, i)
                    if s > 0 and i == 1:
                        take_roots(s - 1)
                    behind = s - 1 if i > 2 else s - 2
                    if 0 <= behind < SPANS - 1:
                        normalize(behind, *((i - 3) * WN, (i - 2) * WN) if i > 2 else ((i + 2) * WN, (i + 3) * WN))
            normalize(SPANS - 1, 0, ACT_SHARE)

_INS = ["x", "src", "dst", "edge_attr_128", "L0_gnn_W_node", "L0_gnn_b_node", "L0_gnn_W_edge", "L0_gnn_b_edge",
        "L0_gnn_W_msg", "L0_gnn_b_msg"]


def kernel(**inputs):
    import numpy as _np
    import concourse.bacc as _bacc
    from concourse import mybir as _mybir
    from concourse.bass_utils import run_bass_kernel_spmd as _run

    nc = _bacc.Bacc("TRN2", target_bir_lowering=False, num_devices=1)
    arrays, args = {}, []
    for name in _INS:
        a = _np.ascontiguousarray(inputs[name])
        arrays[f"in_{name}_dram"] = a
        args.append(nc.dram_tensor(f"in_{name}_dram", a.shape, _mybir.dt.from_np(a.dtype), kind="ExternalInput").ap())
    out = nc.dram_tensor("out_dram", inputs["x"].shape, _mybir.dt.float32, kind="ExternalOutput").ap()
    gnn_layer(nc, *args, out)
    r = _run(nc, [arrays], core_ids=[0])
    return r.results[0]["out_dram"]
```
